# Optimizing a Trainium2 kernel written in Bass

```python
import numpy as np
import jax
import jax.numpy as jnp

def _softmax(x, axis=-1):
    return jax.nn.softmax(x, axis=axis)

def _gelu(x):
    return jax.nn.gelu(x, approximate=True)

def _silu(x):
    return jax.nn.silu(x)

def _sigmoid(x):
    return jax.nn.sigmoid(x)

def _layernorm(x, axis=-1, eps=1e-05):
    m = jnp.mean(x, axis=axis, keepdims=True)
    v = jnp.var(x, axis=axis, keepdims=True)
    return (x - m) / jnp.sqrt(v + eps)

def _scatter_add(tgt, idx, src, axis=0):
    return tgt.at[idx].add(src)

def _segment_sum(src, seg, n):
    return jax.ops.segment_sum(src, seg, n)
kernel_name = 'mk_flamingo_gated_d1_seqx_r4_5ab9d2'

def setup_inputs(seed: int=0):
    np.random.seed(seed)
    _w = jnp.asarray

    def _rec_inputs():
        import jax
        import jax.numpy as jnp
        _rk = jax.random.key(seed)
        x = -0.000125 + 0.9999 * jax.random.normal(jax.random.fold_in(_rk, 1), (2, 512, 1024), jnp.float32)
        _lenS = 512 - jax.random.randint(jax.random.fold_in(_rk, 7), (2,), 0, max(1, 512 // 4) + 1, jnp.int32)
        _lenS2 = 1024 - jax.random.randint(jax.random.fold_in(_rk, 8), (2,), 0, max(1, 1024 // 4) + 1, jnp.int32)
        _ctx_4096P = jax.random.normal(jax.random.fold_in(_rk, 11), (2, 16, 1024), jnp.float32)
        _ctx_4096c = jax.random.dirichlet(jax.random.fold_in(_rk, 511), 0.3 * jnp.ones((16,), jnp.float32), (2, 1024))
        _ctx_4096t = jnp.einsum('bsk,bkd->bsd', _ctx_4096c, _ctx_4096P)
        _ctx_4096t = _ctx_4096t * jax.lax.rsqrt(jnp.mean(jnp.square(_ctx_4096t)) + 1e-12) * 0.953939
        ctx_4096 = -5.72187e-05 + 0.999849 * (_ctx_4096t + 0.3 * jax.random.normal(jax.random.fold_in(_rk, 611), (2, 1024, 1024), jnp.float32))
        _g = jax.random.normal(jax.random.fold_in(_rk, 9001), (2, 1), jnp.float32)
        _g = jnp.sign(_g) * jnp.maximum(jnp.abs(_g), 1.0) + (_g == 0) * 1.0
        g_xattn = _g[0]
        g_ffn = _g[1]
        return (x, ctx_4096, g_xattn, g_ffn)
    x, ctx_4096, g_xattn, g_ffn = _rec_inputs()

    def _L0_xattn_setup():
        import jax, jax.numpy as jnp
        import numpy as np
        QMIN = 0.0
        QMAX = 255.0

        def fake_quant(x, scale, zp):
            s = scale.reshape(())
            z = zp.reshape(())
            q = jnp.clip(jnp.round(x / s + z), QMIN, QMAX)
            return (q - z) * s
        key = jax.random.key(seed)
        k1, k2 = jax.random.split(key)
        B, M, K, N = (4, 512, 1024, 1024)
        x1 = jax.random.normal(k1, (B, M, K), dtype=jnp.float32)
        x2 = jax.random.normal(k2, (B, K, N), dtype=jnp.float32)
        x1_scale = jnp.full((1,), 8.0 / 255.0, dtype=jnp.float32)
        x1_zp = jnp.full((1,), 128.0, dtype=jnp.float32)
        x2_scale = jnp.full((1,), 8.0 / 255.0, dtype=jnp.float32)
        x2_zp = jnp.full((1,), 128.0, dtype=jnp.float32)
        return {'x1': x1, 'x2': x2, 'x1_scale': x1_scale, 'x1_zp': x1_zp, 'x2_scale': x2_scale, 'x2_zp': x2_zp}
    _L0_xattn_all = _L0_xattn_setup()
    _L0_xattn_in = {k: v for k, v in _L0_xattn_all.items() if k in ('x1_scale', 'x1_zp', 'x2_scale', 'x2_zp')}
    del _L0_xattn_all

    def _L0_ffn_setup():
        import jax, jax.numpy as jnp
        import numpy as np

        def sparsemax(z):
            E = z.shape[-1]
            z_sorted = -jnp.sort(-z, axis=-1)
            z_cum = jnp.cumsum(z_sorted, axis=-1)
            k = jnp.arange(1, E + 1, dtype=z.dtype)
            support = 1.0 + k * z_sorted > z_cum
            k_z = jnp.sum(support, axis=-1, keepdims=True)
            tau_sum = jnp.take_along_axis(z_cum, k_z.astype(jnp.int32) - 1, axis=-1)
            tau = (tau_sum - 1.0) / k_z.astype(z.dtype)
            return jnp.maximum(z - tau, 0.0)
        key = jax.random.key(seed)
        ks = jax.random.split(key, 6)
        B, S, D_IN, D_OUT, E, R = (8, 512, 1024, 1024, 8, 16)
        x = jax.random.normal(ks[0], (B, S, D_IN), dtype=jnp.float32)
        W_base = jax.random.normal(ks[1], (D_OUT, D_IN), dtype=jnp.float32) * D_IN ** (-0.5)
        b_base = jax.random.normal(ks[2], (D_OUT,), dtype=jnp.float32) * 0.01
        W_router = jax.random.normal(ks[3], (E, D_IN), dtype=jnp.float32) * D_IN ** (-0.5)
        b_router = jnp.zeros((E,), dtype=jnp.float32)
        lora_A = jax.random.normal(ks[4], (E, D_IN, R), dtype=jnp.float32) * D_IN ** (-0.5)
        lora_B = jnp.zeros((E, R, D_OUT), dtype=jnp.float32)
        return {'x': x, 'W_base': W_base, 'b_base': b_base, 'W_router': W_router, 'b_router': b_router, 'lora_A': lora_A, 'lora_B': lora_B}
    _L0_ffn_all = _L0_ffn_setup()
    _L0_ffn_in = {k: v for k, v in _L0_ffn_all.items() if k in ('W_base', 'b_base', 'W_router', 'b_router', 'lora_A', 'lora_B')}
    del _L0_ffn_all
    return {'x': x, 'ctx_4096': ctx_4096, 'g_xattn': g_xattn, 'g_ffn': g_ffn, 'L0_xattn_x1_scale': _L0_xattn_in['x1_scale'], 'L0_xattn_x1_zp': _L0_xattn_in['x1_zp'], 'L0_xattn_x2_scale': _L0_xattn_in['x2_scale'], 'L0_xattn_x2_zp': _L0_xattn_in['x2_zp'], 'L0_ffn_W_base': _L0_ffn_in['W_base'], 'L0_ffn_b_base': _L0_ffn_in['b_base'], 'L0_ffn_W_router': _L0_ffn_in['W_router'], 'L0_ffn_b_router': _L0_ffn_in['b_router'], 'L0_ffn_lora_A': _L0_ffn_in['lora_A'], 'L0_ffn_lora_B': _L0_ffn_in['lora_B']}

def reference(x, ctx_4096, g_xattn, g_ffn, L0_xattn_x1_scale, L0_xattn_x1_zp, L0_xattn_x2_scale, L0_xattn_x2_zp, L0_ffn_W_base, L0_ffn_b_base, L0_ffn_W_router, L0_ffn_b_router, L0_ffn_lora_A, L0_ffn_lora_B):
    import jax
    import jax.numpy as jnp

    def _L0_xattn_ref(x1, x2, x1_scale, x1_zp, x2_scale, x2_zp):
        import jax, jax.numpy as jnp
        import numpy as np
        QMIN = 0.0
        QMAX = 255.0

        def fake_quant(x, scale, zp):
            s = scale.reshape(())
            z = zp.reshape(())
            q = jnp.clip(jnp.round(x / s + z), QMIN, QMAX)
            return (q - z) * s
        q1 = fake_quant(x1, x1_scale, x1_zp)
        q2 = fake_quant(x2, x2_scale, x2_zp)
        return jnp.matmul(q1, q2)

    def _L0_ffn_ref(x, W_base, b_base, W_router, b_router, lora_A, lora_B):
        import jax, jax.numpy as jnp
        import numpy as np

        def sparsemax(z):
            E = z.shape[-1]
            z_sorted = -jnp.sort(-z, axis=-1)
            z_cum = jnp.cumsum(z_sorted, axis=-1)
            k = jnp.arange(1, E + 1, dtype=z.dtype)
            support = 1.0 + k * z_sorted > z_cum
            k_z = jnp.sum(support, axis=-1, keepdims=True)
            tau_sum = jnp.take_along_axis(z_cum, k_z.astype(jnp.int32) - 1, axis=-1)
            tau = (tau_sum - 1.0) / k_z.astype(z.dtype)
            return jnp.maximum(z - tau, 0.0)
        base_out = jnp.einsum('bsd,od->bso', x, W_base) + b_base
        logits = jnp.einsum('bsd,ed->bse', x, W_router) + b_router
        weights = sparsemax(logits)
        h = jnp.einsum('bsd,edr->bser', x, lora_A)
        expert_out = jnp.einsum('bser,bse,ero->bso', h, weights, lora_B)
        return base_out + expert_out
    x = x + jnp.tanh(g_xattn[0]) * _L0_xattn_ref(_layernorm(x, axis=-1), ctx_4096, L0_xattn_x1_scale, L0_xattn_x1_zp, L0_xattn_x2_scale, L0_xattn_x2_zp)
    x = x + jnp.tanh(g_ffn[0]) * _L0_ffn_ref(_layernorm(x, axis=-1), L0_ffn_W_base, L0_ffn_b_base, L0_ffn_W_router, L0_ffn_b_router, L0_ffn_lora_A, L0_ffn_lora_B)
    return x

_drawn_inputs = setup_inputs


def setup_inputs(seed=0):
    import zlib

    import numpy as np

    out = dict(_drawn_inputs(seed))
    spreads = {'L0_ffn_b_router': (0.0, 0.8), 'L0_ffn_lora_B': (0.0, 0.572)}
    factors = {'L0_ffn_b_base': 64.0, 'L0_ffn_W_router': 4.44, 'L0_ffn_lora_A': 4.023}
    for name, (base, spread) in spreads.items():
        noise = np.random.default_rng([zlib.crc32(name.encode()), seed]).standard_normal(out[name].shape)
        drawn = base * np.exp(spread * noise) if base else spread * noise
        out[name] = jnp.asarray(drawn.astype(out[name].dtype))
    for name, factor in factors.items():
        out[name] = (out[name] * factor).astype(out[name].dtype)
    return out
```

```python
import concourse.bass as bass
from concourse import mybir
from contextlib import ExitStack

FP32 = mybir.dt.float32
FP32R = mybir.dt.float32r
FP16 = mybir.dt.float16
UINT8 = mybir.dt.uint8
INT32 = mybir.dt.int32
ALU = mybir.AluOpType
ACT = mybir.ActivationFunctionType
AX = mybir.AxisListType

P = 128
HALF = 512
EPS = 1e-5
MID = 128.0
RSQRT_SEED = 0x5F3759DF
N_SCALARS = 6
RING = 6


def flamingo_layer(nc, x, ctx, scalars, wT, b_base, ar, lora_b, out):
    B, S, D = x.shape
    KC = D // P
    TILES = B * S // P
    TPB = S // P
    PAIRS = TILES // 2
    NH = D // HALF
    ARW = ar.shape[1]
    ER = lora_b.shape[0]
    E = ARW - ER
    R = ER // E

    x_rows = x.rearrange("b (t p) d -> p (b t) d", p=P)
    out_rows = out.rearrange("b (t p) d -> p (b t) d", p=P)
    ctx_rows = ctx.rearrange("b (k p) n -> p b k n", p=P)
    wT_rows = wT.rearrange("(k p) o -> p k o", p=P)
    ar_rows = ar.rearrange("(k p) c -> p k c", p=P)

    KP = KC // 2
    items = [("ctx", 0, k) for k in range(KC)] + [("ctx", 1, k) for k in range(KC)]
    items += [("ar", 0, 0), ("ar", 1, 0)] + [("w", 0, kp) for kp in range(KP)] + [("lb", 0, 0)]
    items += [("w", 1, kp) for kp in range(KP)]
    FIRST_W = B * KC
    N_W = len(items) - FIRST_W

    with ExitStack() as stack:
        def sb(name, shape, dt):
            return stack.enter_context(nc.sbuf_tensor(name, shape, dt))

        def pb(name, shape, dt):
            return stack.enter_context(nc.psum_tensor(name, shape, dt))

        def sem(name):
            return stack.enter_context(nc.semaphore(name))

        xs = sb("xs", [P, TILES, D], FP32)
        ring = sb("ring", [P, RING, D], FP32)
        ctx_u8 = sb("ctx_u8", [P, 2, D], UINT8)
        ctxq = sb("ctxq", [P, B, KC, D], FP16)
        q_u8 = sb("q_u8", [P, 2, D], UINT8)
        q_16 = sb("q_16", [P, 2, D], FP16)
        qT = sb("qT", [P, 2, KC, P], FP16)
        col_term = sb("col_term", [P, B, D], FP32)
        w_hi = sb("w_hi", [P, KC, D], FP32R)
        w_lo = sb("w_lo", [P, KC, D], FP32R)
        ar_hi = sb("ar_hi", [P, KC, ARW], FP32R)
        ar_lo = sb("ar_lo", [P, KC, ARW], FP32R)
        lb_hi = sb("lb_hi", [P, D], FP32R)
        lb_lo = sb("lb_lo", [P, D], FP32R)
        xT_hi = sb("xT_hi", [P, 2, KC, P], FP32R)
        xT_lo = sb("xT_lo", [P, 2, KC, P], FP32R)
        hwT_hi = sb("hwT_hi", [P, P], FP32R)
        hwT_lo = sb("hwT_lo", [P, P], FP32R)
        late = ctxq[:, 0, :, :].rearrange("p k n -> p (k n)").bitcast(FP32)
        xn = late[:, 0:2 * D].rearrange("p (i d) -> p i d", i=2)
        bias = late[:, 2 * D:3 * D]
        hw = late[:, 3 * D:3 * D + ER]
        ident16 = sb("ident16", [P, P], FP16)
        ident32 = sb("ident32", [P, P], FP32)
        ones16 = sb("ones16", [P, P], FP16)
        sc = sb("sc", [P, N_SCALARS + E], FP32)
        cc = sb("cc", [P, 12], FP32)
        th = sb("th", [P, 2], FP32)
        inv_k = sb("inv_k", [P, E], FP32)
        ones_e = sb("ones_e", [P, E], FP32)
        rowsum = sb("rowsum", [P, TILES], FP32)
        row_term = sb("row_term", [P, 2], FP32)
        stats = sb("stats", [P, 2, 2, 6], FP32)
        mv = sb("mv", [P, 2, 2], FP32)
        var_e = sb("var_e", [P, 2], FP32)
        rs = sb("rs", [P, 2], FP32)
        nt = sb("nt", [P, 2], FP32)
        half_bits = sb("half_bits", [P, 2], INT32)
        qa = sb("qa", [P, 2], FP32)
        qm = sb("qm", [P, 2], FP32)
        lg = sb("lg", [P, E], FP32)
        lg_sorted = sb("lg_sorted", [P, E], FP32)
        cum = sb("cum", [P, E], FP32)
        cand = sb("cand", [P, E], FP32)
        tau = sb("tau", [P, 1], FP32)
        ew = sb("ew", [P, E], FP32)

        S1, Z1, S2, Z2 = (sc[:, i:i + 1] for i in range(4))
        b_router = sc[:, N_SCALARS:N_SCALARS + E]
        INV1, INV2, NZ1, C, D1, D2, CD1, CD2, NKZ1, SS = (cc[:, i:i + 1] for i in range(10))
        TX, TF = th[:, 0:1], th[:, 1:2]

        acc = [[pb(f"acc{s}{n}", [P, HALF], FP32) for n in range(NH)] for s in range(2)]
        xbank = [pb(f"xbank{n}", [P, HALF], FP32) for n in range(NH)]
        qbank = pb("qbank", [P, KC, P], FP16)
        hbank = pb("hbank", [P, HALF], FP32)
        h_psum, lg_psum, hwT_psum = hbank[:, 0:ER], hbank[:, ER:ARW], hbank[:, 256:256 + P]

        small_in = sem("small_in")
        x_in = [sem(f"x_in{p}") for p in range(PAIRS)]
        ring_in = [sem(f"ring_in{s}") for s in range(RING)]
        tanh_ready = sem("tanh_ready")
        consts_ready = sem("consts_ready")
        ident_zero = sem("ident_zero")
        ident_ready = sem("ident_ready")
        bias_ready = sem("bias_ready")
        vec = sem("vec")
        ctx_rounded = [sem("ctx_rounded0"), sem("ctx_rounded1")]
        ctx_ready = sem("ctx_ready")
        q_rounded = sem("q_rounded")
        q16_ready = sem("q16_ready")
        q_turned = sem("q_turned")
        qT_ready = sem("qT_ready")
        attn_half = sem("attn_half")
        attn_added = sem("attn_added")
        colsum_done = sem("colsum_done")
        col_ready = sem("col_ready")
        w_hi_done = sem("w_hi_done")
        w_lo_done = sem("w_lo_done")
        xn_ready = sem("xn_ready")
        biased = sem("biased")
        x_turned = sem("x_turned")
        xT_hi_done = sem("xT_hi_done")
        xT_lo_done = sem("xT_lo_done")
        ar_done = sem("ar_done")
        hw_ready = sem("hw_ready")
        hw_turned = sem("hw_turned")
        hwT_hi_done = sem("hwT_hi_done")
        hwT_lo_done = sem("hwT_lo_done")
        ffn_half = sem("ffn_half")
        out_half = sem("out_half")
        stored = sem("stored")

        block = stack.enter_context(nc.Block())

        def ring_ready(eng, i):
            eng.wait_ge(ring_in[i % RING], 16 * (i // RING + 1))

        def ring_view(i):
            kind = items[i][0]
            slot = ring[:, i % RING]
            return slot[:, 0:KC // 2 * ARW] if kind == "ar" else slot

        def split_out(i, hi, lo):
            kind, n, kp = items[i]
            if kind == "ar":
                ks = slice(n * KC // 2, (n + 1) * KC // 2)
                return hi["ar"][:, ks, :], lo["ar"][:, ks, :]
            if kind == "lb":
                return hi["lb"][:, :], lo["lb"][:, :]
            at = (slice(None), slice(2 * kp, 2 * kp + 2), slice(n * HALF, (n + 1) * HALF))
            return hi["w"][at], lo["w"][at]

        def ring_parts(i):
            kind = items[i][0]
            if kind == "ar":
                return ring_view(i).rearrange("p (k c) -> p k c", c=ARW)
            if kind == "lb":
                return ring_view(i)
            return ring_view(i).rearrange("p (k c) -> p k c", c=HALF)

        HI = {"w": w_hi, "ar": ar_hi, "lb": lb_hi}
        LO = {"w": w_lo, "ar": ar_lo, "lb": lb_lo}
        LB_ITEM = FIRST_W + 2 + KP

        def w_item(n, kp):
            return FIRST_W + 2 + kp if n == 0 else FIRST_W + 3 + KP + kp

        @block.sync
        def _(sp):
            sp.dma_start(sc[:, :], scalars).then_inc(small_in, 16)
            sp.dma_start(xs[:, 0:2, :], x_rows[:, 0:2, :]).then_inc(x_in[0], 16)
            for i, (kind, a, b) in enumerate(items):
                j = i - RING
                if j >= FIRST_W:
                    sp.wait_ge(w_lo_done, j - FIRST_W + 1)
                elif j >= 0:
                    sp.wait_ge(ctx_rounded[j // KC], j % KC + 1)
                dst = ring_parts(i)
                if kind == "ctx":
                    dst, src = ring_view(i), ctx_rows[:, a, b, :]
                elif kind == "ar":
                    src = ar_rows[:, a * KC // 2:(a + 1) * KC // 2, :]
                elif kind == "lb":
                    src = lora_b
                else:
                    src = wT_rows[:, 2 * b:2 * b + 2, a * HALF:(a + 1) * HALF]
                sp.dma_start(dst, src).then_inc(ring_in[i % RING], 16)
                if i in (3, KC + 1, KC + 5):
                    p = {3: 1, KC + 1: 2, KC + 5: 3}[i]
                    sp.dma_start(xs[:, 2 * p:2 * p + 2, :], x_rows[:, 2 * p:2 * p + 2, :]).then_inc(x_in[p], 16)
                if i == FIRST_W:
                    sp.wait_ge(attn_half, NH * TPB)
                    sp.dma_start(bias[:, :], b_base.partition_broadcast(P)).then_inc(small_in, 16)
            for t in range(TILES):
                for n in range(NH):
                    cols = slice(n * HALF, (n + 1) * HALF)
                    sp.wait_ge(out_half, NH * t + n + 1)
                    sp.dma_start(out_rows[:, t, cols], xs[:, t, cols]).then_inc(stored, 16)
            sp.wait_ge(stored, 16 * TILES * NH)

        @block.gpsimd
        def _(pool):
            pool.memset(ident16[:, :], 0.0).then_inc(ident_zero, 1)
            pool.memset(ident32[:, :], 0.0).then_inc(ident_zero, 1)
            pool.memset(ones16[:, :], 1.0).then_inc(ident_ready, 1)
            pool.wait_ge(ident_zero, 2)
            for m in (ident16, ident32):
                pool.affine_select(out=m[:, :], in_=m[:, :], compare_op=ALU.not_equal, fill=1.0, base=0,
                                   pattern=[[-1, P]], channel_multiplier=1).then_inc(ident_ready, 1)
            for b in range(B):
                for k in range(KC):
                    pool.wait_ge(ctx_rounded[b], k + 1)
                    pool.tensor_scalar(ctxq[:, b, k, :], ctx_u8[:, k % 2, :], 1.0, -MID, ALU.mult, ALU.add)\
                        .then_inc(ctx_ready, 1)
            for i in range(FIRST_W, len(items)):
                hi, lo = split_out(i, HI, LO)
                pool.wait_ge(w_hi_done, i - FIRST_W + 1)
                pool.tensor_tensor(lo, ring_parts(i), hi.bitcast(FP32), ALU.subtract).then_inc(w_lo_done, 1)
            pool.wait_ge(bias_ready, 1)
            for t in range(TILES):
                pool.wait_ge(xn_ready, t + 1)
                pool.tensor_tensor(xs[:, t, :], xs[:, t, :], bias[:, :], ALU.add).then_inc(biased, 1)

        @block.scalar
        def _(act):
            act.wait_ge(small_in, 16)
            act.activation(th[:, :], sc[:, 4:6], ACT.Tanh).then_inc(tanh_ready, 1)

            def q_to_16(t):
                act.wait_ge(q_rounded, t + 1)
                if t >= 2:
                    act.wait_ge(q_turned, t - 1)
                act.activation(q_16[:, t % 2, :], q_u8[:, t % 2, :], ACT.Copy,
                               accum_out=rowsum[:, t:t + 1]).then_inc(q16_ready, 1)

            def q_out(t):
                act.wait_ge(q_turned, t + 1)
                if t >= 2:
                    act.wait_ge(attn_half, NH * (t - 1))
                act.activation(qT[:, t % 2, :, :], qbank[:, :, :], ACT.Copy, bias=-MID).then_inc(qT_ready, 1)

            def col_out(b):
                act.wait_ge(colsum_done, b + 1)
                for n in range(NH):
                    act.activation(col_term[:, b, n * HALF:(n + 1) * HALF], xbank[n][:, :], ACT.Copy, scale=CD1)\
                       .then_inc(col_ready, 1)

            def round_ctx(b, k):
                i = b * KC + k
                ring_ready(act, i)
                act.wait_ge(ctx_ready, i - 1)
                act.activation(ctx_u8[:, k % 2, :], ring_view(i), ACT.Identity, bias=Z2, scale=INV2)\
                   .then_inc(ctx_rounded[b], 1)

            def high_part(i):
                hi, _ = split_out(i, HI, LO)
                ring_ready(act, i)
                act.activation(hi, ring_parts(i), ACT.Copy).then_inc(w_hi_done, 1)

            act.wait_ge(consts_ready, 1)
            q_to_16(0)
            q_to_16(1)
            q_out(0)
            q_out(1)
            q_to_16(2)
            q_to_16(3)
            col_out(0)
            q_out(2)
            for k in range(KC // 2):
                round_ctx(1, k)
            q_out(3)
            for k in range(KC // 2, KC):
                round_ctx(1, k)
            for t in (4, 5):
                q_to_16(t)
            for t in (4, 5):
                q_out(t)
            q_to_16(6)
            q_to_16(7)
            col_out(1)
            q_out(6)
            for i in range(FIRST_W, FIRST_W + 3):
                high_part(i)
            q_out(7)

            def xT_high(t):
                for n in range(NH):
                    act.wait_ge(x_turned, NH * t + n + 1)
                    act.activation(xT_hi[:, t % 2, n * 4:(n + 1) * 4, :],
                                   xbank[n][:, :].rearrange("p (k c) -> p k c", c=P), ACT.Copy)\
                       .then_inc(xT_hi_done, 1)

            def hwT_high(t):
                act.wait_ge(hw_turned, t + 1)
                act.activation(hwT_hi[:, :], hwT_psum, ACT.Copy).then_inc(hwT_hi_done, 1)

            for i in range(FIRST_W + 3, LB_ITEM + 1):
                high_part(i)
            xT_high(0)
            for i in range(LB_ITEM + 1, len(items)):
                high_part(i)
            for t in range(TILES):
                hwT_high(t)
                if t + 1 < TILES:
                    xT_high(t + 1)

        @block.vector
        def _(dve):
            step = [0]

            def then_wait(ins):
                step[0] += 1
                ins.then_inc(vec, 1)
                dve.wait_ge(vec, step[0])

            for e in range(E):
                dve.memset(inv_k[:, e:e + 1], 1.0 / (e + 1))
            dve.memset(ones_e[:, :], 1.0)
            dve.wait_ge(small_in, 16)
            dve.wait_ge(tanh_ready, 1)
            dve.reciprocal(INV1, S1)
            dve.reciprocal(INV2, S2)
            dve.tensor_scalar(NZ1, Z1, -1.0, None, ALU.mult)
            dve.tensor_scalar(D1, Z1, -1.0, MID, ALU.mult, ALU.add)
            dve.tensor_scalar(D2, Z2, -1.0, MID, ALU.mult, ALU.add)
            dve.tensor_scalar(NKZ1, Z1, -float(D), None, ALU.mult)
            then_wait(dve.tensor_tensor(SS, S1, S2, ALU.mult))
            then_wait(dve.tensor_tensor(C, SS, TX, ALU.mult))
            dve.tensor_tensor(CD1, C, D1, ALU.mult)
            then_wait(dve.tensor_tensor(CD2, C, D2, ALU.mult))
            dve.tensor_copy(tau[:, :], CD2).then_inc(consts_ready, 1)

            def moments():
                then_wait(dve.tensor_scalar(var_e[:, :], mv[:, :, 1], EPS, None, ALU.add))
                then_wait(dve.tensor_scalar(half_bits[:, :], var_e[:, :].bitcast(INT32), 1, None,
                                            ALU.logical_shift_right))
                then_wait(dve.tensor_scalar(rs[:, :].bitcast(INT32), half_bits[:, :], -1.0, float(RSQRT_SEED),
                                            ALU.mult, ALU.add))
                for _ in range(3):
                    then_wait(dve.tensor_tensor(nt[:, :], rs[:, :], rs[:, :], ALU.mult))
                    then_wait(dve.scalar_tensor_tensor(nt[:, :], nt[:, :], -0.5, var_e[:, :], ALU.mult, ALU.mult))
                    then_wait(dve.scalar_tensor_tensor(rs[:, :], nt[:, :], 1.5, rs[:, :], ALU.add, ALU.mult))

            def pair_stats(t0):
                for i in range(2):
                    for n in range(NH):
                        ins = dve.bn_stats(stats[:, i, n, :], xs[:, t0 + i, n * HALF:(n + 1) * HALF])
                then_wait(ins)
                for i in range(2):
                    ins = dve.bn_aggr(mv[:, i, :], stats[:, i, :, :].rearrange("p n s -> p (n s)"))
                then_wait(ins)
                moments()

            def quantise_pair(p):
                dve.wait_ge(x_in[p], 16)
                pair_stats(2 * p)
                then_wait(dve.tensor_scalar(qa[:, :], rs[:, :], INV1, None, ALU.mult))
                then_wait(dve.reciprocal(nt[:, :], qa[:, :]))
                then_wait(dve.scalar_tensor_tensor(qm[:, :], nt[:, :], NZ1, mv[:, :, 0], ALU.mult, ALU.add))
                for i in range(2):
                    t = 2 * p + i
                    if t >= 2:
                        dve.wait_ge(q16_ready, t - 1)
                    dve.tensor_scalar(q_u8[:, i, :], xs[:, t, :], qm[:, i:i + 1], qa[:, i:i + 1],
                                      ALU.subtract, ALU.mult).then_inc(q_rounded, 1)

            def round_ctx(k):
                ring_ready(dve, k)
                if k >= 2:
                    dve.wait_ge(ctx_ready, k - 1)
                dve.tensor_scalar(ctx_u8[:, k % 2, :], ring_view(k), INV2, Z2, ALU.mult, ALU.add)\
                   .then_inc(ctx_rounded[0], 1)

            def add_attention(t):
                for n in range(NH):
                    cols = slice(n * HALF, (n + 1) * HALF)
                    dve.wait_ge(attn_half, NH * t + n + 1)
                    dve.scalar_tensor_tensor(xs[:, t, cols], acc[t % 2][n][:, :], C, xs[:, t, cols],
                                             ALU.mult, ALU.add).then_inc(attn_added, 1)

            def norm_pair(p):
                b = 2 * p // TPB
                dve.wait_ge(q16_ready, 2 * p + 2)
                dve.wait_ge(col_ready, NH * (b + 1))
                then_wait(dve.tensor_scalar(row_term[:, :], rowsum[:, 2 * p:2 * p + 2], NKZ1, CD2,
                                            ALU.add, ALU.mult))
                for i in range(2):
                    ins = dve.scalar_tensor_tensor(xs[:, 2 * p + i, :], xs[:, 2 * p + i, :], row_term[:, i:i + 1],
                                                   col_term[:, b, :], ALU.add, ALU.add)
                then_wait(ins)
                pair_stats(2 * p)
                if p:
                    dve.wait_ge(x_turned, NH * 2 * p)
                else:
                    dve.wait_ge(attn_half, NH * TPB)
                for i in range(2):
                    dve.tensor_scalar(xn[:, i, :], xs[:, 2 * p + i, :], mv[:, i, 0:1], rs[:, i:i + 1],
                                      ALU.subtract, ALU.mult).then_inc(xn_ready, 1)

            def xT_low(t):
                for n in range(NH):
                    dve.wait_ge(xT_hi_done, NH * t + n + 1)
                    dve.tensor_tensor(xT_lo[:, t % 2, n * 4:(n + 1) * 4, :],
                                      xbank[n][:, :].rearrange("p (k c) -> p k c", c=P),
                                      xT_hi[:, t % 2, n * 4:(n + 1) * 4, :].bitcast(FP32), ALU.subtract)\
                       .then_inc(xT_lo_done, 1)

            def route(t):
                dve.wait_ge(ar_done, t + 1)
                then_wait(dve.tensor_tensor(lg[:, :], lg_psum, b_router, ALU.add))
                then_wait(dve.max(lg_sorted[:, :], lg[:, :]))
                then_wait(dve.tensor_tensor_scan(cum[:, :], ones_e[:, :], lg_sorted[:, :], -1.0,
                                                 ALU.mult, ALU.add))
                then_wait(dve.tensor_tensor(cand[:, :], cum[:, :], inv_k[:, :], ALU.mult))
                then_wait(dve.reduce_max(tau[:, :], cand[:, :], AX.X))
                then_wait(dve.tensor_scalar(ew[:, :], lg[:, :], tau[:, 0:1], 0.0, ALU.subtract, ALU.max))
                dve.tensor_tensor(hw[:, :].rearrange("p (e r) -> p e r", r=R),
                                  h_psum.rearrange("p (e r) -> p e r", r=R),
                                  ew[:, :].unsqueeze(2).to_broadcast([P, E, R]), ALU.mult).then_inc(hw_ready, 1)

            def hwT_low(t):
                dve.wait_ge(hwT_hi_done, t + 1)
                dve.tensor_tensor(hwT_lo[:, :], hwT_psum, hwT_hi[:, :].bitcast(FP32), ALU.subtract)\
                   .then_inc(hwT_lo_done, 1)

            def add_layer(t, n):
                cols = slice(n * HALF, (n + 1) * HALF)
                if n == 0:
                    dve.wait_ge(biased, t + 1)
                dve.wait_ge(ffn_half, NH * t + n + 1)
                dve.scalar_tensor_tensor(xs[:, t, cols], acc[t % 2][n][:, :], TF, xs[:, t, cols],
                                         ALU.mult, ALU.add).then_inc(out_half, 1)

            quantise_pair(0)
            for k in range(KC // 2):
                round_ctx(k)
            quantise_pair(1)
            for k in range(KC // 2, KC):
                round_ctx(k)
            add_attention(0)
            add_attention(1)
            quantise_pair(2)
            add_attention(2)
            add_attention(3)
            norm_pair(0)
            quantise_pair(3)
            dve.wait_ge(small_in, 32)
            dve.tensor_scalar(bias[:, :], bias[:, :], TF, None, ALU.mult).then_inc(bias_ready, 1)
            for t in range(TPB, TILES):
                add_attention(t)
                if t == 5:
                    xT_low(0)
            for t in range(TILES):
                route(t)
                hwT_low(t)
                add_layer(t, 0)
                if t + 1 < TILES:
                    xT_low(t + 1)
                if t % 2 == 0 and t + 2 < TILES:
                    norm_pair(t // 2 + 1)
                add_layer(t, 1)

        @block.tensor
        def _(pe):
            pe.wait_ge(ident_ready, 3)

            def turn_q(t):
                pe.wait_ge(q16_ready, t + 1)
                if t:
                    pe.wait_ge(qT_ready, t)
                for k in range(KC):
                    ins = pe.transpose(qbank[:, k, :], q_16[:, t % 2, k * P:(k + 1) * P], ident16[:, :])
                ins.then_inc(q_turned, 1)

            def attend(t, n, k):
                return pe.matmul(acc[t % 2][n][:, :], qT[:, t % 2, k, :],
                                 ctxq[:, t // TPB, k, n * HALF:(n + 1) * HALF], start=(k == 0), stop=(k == KC - 1))

            def attend_first(b):
                t = b * TPB
                pe.wait_ge(qT_ready, t + 1)
                if t >= 2:
                    pe.wait_ge(attn_added, NH * (t - 1))
                if b:
                    pe.wait_ge(col_ready, NH * b)
                for k in range(KC):
                    pe.wait_ge(ctx_ready, b * KC + k + 1)
                    for n in range(NH):
                        col = pe.matmul(xbank[n][:, :], ones16[:, :], ctxq[:, b, k, n * HALF:(n + 1) * HALF],
                                        start=(k == 0), stop=(k == KC - 1))
                    if k == KC - 1:
                        col.then_inc(colsum_done, 1)
                    for n in range(NH):
                        ins = attend(t, n, k)
                        if k == KC - 1:
                            ins.then_inc(attn_half, 1)

            def attend_tile(t):
                pe.wait_ge(qT_ready, t + 1)
                if t >= 2:
                    pe.wait_ge(attn_added, NH * (t - 1))
                for n in range(NH):
                    for k in range(KC):
                        ins = attend(t, n, k)
                    ins.then_inc(attn_half, 1)

            def turn_x(t):
                pe.wait_ge(xn_ready, t + 1)
                if t:
                    pe.wait_ge(xT_lo_done, NH * t)
                else:
                    pe.wait_ge(col_ready, NH * B)
                for k in range(KC):
                    ins = pe.transpose(xbank[k // 4][:, k % 4 * P:(k % 4 + 1) * P],
                                       xn[:, t % 2, k * P:(k + 1) * P], ident32[:, :])
                    if k % 4 == 3:
                        ins.then_inc(x_turned, 1)

            def passes(hi, lo):
                return ((hi[0], hi[1]), (hi[0], lo[1]), (lo[0], hi[1]))

            def project(t):
                pe.wait_ge(xT_lo_done, NH * (t + 1))
                if t == 0:
                    pe.wait_ge(w_lo_done, 2)
                for k in range(KC):
                    xh, xl = xT_hi[:, t % 2, k, :], xT_lo[:, t % 2, k, :]
                    for a, (l, r) in enumerate(((xl, ar_hi), (xh, ar_lo), (xh, ar_hi))):
                        ins = pe.matmul(hbank[:, 0:ARW], l, r[:, k, :], start=(k == 0 and a == 0),
                                        stop=(k == KC - 1 and a == 2))
                ins.then_inc(ar_done, 1)

            def base(t, n, ks):
                for k in ks:
                    if t == 0 and k % 2 == 0:
                        pe.wait_ge(w_lo_done, w_item(n, k // 2) - FIRST_W + 1)
                    xh, xl = xT_hi[:, t % 2, k, :], xT_lo[:, t % 2, k, :]
                    cols = slice(n * HALF, (n + 1) * HALF)
                    for a, (l, r) in enumerate(((xl, w_hi), (xh, w_lo), (xh, w_hi))):
                        pe.matmul(acc[t % 2][n][:, :], l, r[:, k, cols], start=(k == 0 and a == 0), stop=False)

            def experts(t, n):
                if n == 0:
                    pe.wait_ge(hwT_lo_done, t + 1)
                    if t == 0:
                        pe.wait_ge(w_lo_done, LB_ITEM - FIRST_W + 1)
                cols = slice(n * HALF, (n + 1) * HALF)
                for a, (l, r) in enumerate(((hwT_lo, lb_hi), (hwT_hi, lb_lo), (hwT_hi, lb_hi))):
                    ins = pe.matmul(acc[t % 2][n][:, :], l[:, :], r[:, cols], start=False, stop=(a == 2))
                ins.then_inc(ffn_half, 1)

            turn_q(0)
            turn_q(1)
            attend_first(0)
            turn_q(2)
            attend_tile(1)
            turn_q(3)
            attend_tile(2)
            turn_q(4)
            attend_tile(3)
            turn_q(5)
            attend_first(1)
            turn_q(6)
            attend_tile(5)
            turn_q(7)
            turn_x(0)
            attend_tile(6)
            attend_tile(7)
            MIDK = 5
            for t in range(TILES):
                if t < 2:
                    pe.wait_ge(attn_added, NH * (TILES - 1 + t))
                else:
                    pe.wait_ge(out_half, NH * (t - 1))
                project(t)
                base(t, 0, range(MIDK))
                pe.wait_ge(hw_ready, t + 1)
                pe.transpose(hwT_psum, hw[:, :], ident32[:, :]).then_inc(hw_turned, 1)
                base(t, 0, range(MIDK, KC))
                experts(t, 0)
                if t + 1 < TILES:
                    turn_x(t + 1)
                base(t, 1, range(KC))
                experts(t, 1)


def kernel(x, ctx_4096, g_xattn, g_ffn, L0_xattn_x1_scale, L0_xattn_x1_zp, L0_xattn_x2_scale, L0_xattn_x2_zp,
           L0_ffn_W_base, L0_ffn_b_base, L0_ffn_W_router, L0_ffn_b_router, L0_ffn_lora_A, L0_ffn_lora_B):
    import numpy as np
    import concourse.bacc as bacc
    from concourse.bass_utils import run_bass_kernel_spmd

    x = np.asarray(x)
    w_base, router = np.asarray(L0_ffn_W_base), np.asarray(L0_ffn_W_router)
    lora_a, lora_b = np.asarray(L0_ffn_lora_A), np.asarray(L0_ffn_lora_B)
    d_in = w_base.shape[1]
    scalars = np.concatenate([np.asarray(a).reshape(-1) for a in (
        L0_xattn_x1_scale, L0_xattn_x1_zp, L0_xattn_x2_scale, L0_xattn_x2_zp, g_xattn, g_ffn, L0_ffn_b_router)])
    arrays = {
        "x": x,
        "ctx": np.asarray(ctx_4096),
        "scalars": np.tile(scalars, (128, 1)),
        "wT": np.ascontiguousarray(w_base.T),
        "b_base": np.asarray(L0_ffn_b_base),
        "ar": np.ascontiguousarray(np.concatenate(
            [lora_a.transpose(1, 0, 2).reshape(d_in, -1), router.T], axis=1)),
        "lora_b": np.ascontiguousarray(lora_b.reshape(-1, lora_b.shape[-1])),
    }
    nc = bacc.Bacc("TRN2", target_bir_lowering=False, num_devices=1)
    args = [nc.dram_tensor(f"in_{name}", a.shape, mybir.dt.from_np(a.dtype), kind="ExternalInput").ap()
            for name, a in arrays.items()]
    out = nc.dram_tensor("out_y", x.shape, mybir.dt.from_np(x.dtype), kind="ExternalOutput").ap()
    flamingo_layer(nc, *args, out)
    r = run_bass_kernel_spmd(nc, [{f"in_{name}": a for name, a in arrays.items()}], core_ids=[0])
    return r.results[0]["out_y"]
```

```python
import concourse.bass as bass
from concourse import mybir
from contextlib import ExitStack

FP32 = mybir.dt.float32
FP32R = mybir.dt.float32r
FP16 = mybir.dt.float16
UINT8 = mybir.dt.uint8
INT32 = mybir.dt.int32
ALU = mybir.AluOpType
ACT = mybir.ActivationFunctionType
AX = mybir.AxisListType

P = 128
HALF = 512
EPS = 1e-5
MID = 128.0
N_SCALARS = 6
RING = 6


def flamingo_layer(nc, x, ctx, scalars, weights, b_base, lora_b, out):
    B, S, D = x.shape
    KC = D // P
    TILES = B * S // P
    TPB = S // P
    PAIRS = TILES // 2
    NH = D // HALF
    WC = weights.shape[1]
    ARW = WC - D
    ER = lora_b.shape[0]
    E = ARW - ER
    R = ER // E

    WIDE = 400
    CUTS = [0, WC - 2 * WIDE, WC - WIDE, WC]
    G = len(CUTS) - 1
    FIRST, SECOND, THIRD = range(G)
    HWT_AT = HALF - P
    assert CUTS[1] <= HWT_AT and ARW < CUTS[1]

    def group_cols(g):
        at = max(CUTS[g], ARW)
        return slice(at - ARW, CUTS[g + 1] - ARW), slice(at - CUTS[g], CUTS[g + 1] - CUTS[g])

    x_rows = x.rearrange("b (t p) d -> p (b t) d", p=P)
    out_rows = out.rearrange("b (t p) d -> p (b t) d", p=P)
    ctx_rows = ctx.rearrange("b (k p) n -> p b k n", p=P)
    w_rows = weights.rearrange("(k p) c -> p k c", p=P)

    KP = KC // 2
    items = [("ctx", b, k) for b in range(B) for k in range(KC)]
    items += [("w", g, kp) for g in (FIRST, SECOND) for kp in range(KP)]
    items += [("lb", 0, 0)] + [("w", THIRD, kp) for kp in range(KP)]
    FIRST_W = B * KC
    N_W = len(items) - FIRST_W
    BY_VECTOR = KP + 2

    with ExitStack() as stack:
        def sb(name, shape, dt):
            return stack.enter_context(nc.sbuf_tensor(name, shape, dt))

        def pb(name, shape, dt):
            return stack.enter_context(nc.psum_tensor(name, shape, dt))

        def sem(name):
            return stack.enter_context(nc.semaphore(name))

        xs = sb("xs", [P, TILES, D], FP32)
        ring = sb("ring", [P, RING, D], FP32)
        ctx_u8 = sb("ctx_u8", [P, 2, D], UINT8)
        ctxq = sb("ctxq", [P, B, KC, D], FP16)
        q_u8 = sb("q_u8", [P, 2, D], UINT8)
        q_16 = sb("q_16", [P, 2, D], FP16)
        qT = sb("qT", [P, 2, KC, P], FP16)
        col_term = sb("col_term", [P, B, D], FP32)
        w_hi = sb("w_hi", [P, KC, WC], FP32R)
        w_lo = sb("w_lo", [P, KC, WC], FP32R)
        lb_hi = sb("lb_hi", [P, D], FP32R)
        lb_lo = sb("lb_lo", [P, D], FP32R)
        xT_hi = sb("xT_hi", [P, 2, KC, P], FP32R)
        xT_lo = sb("xT_lo", [P, 2, KC, P], FP32R)
        hwT_hi = sb("hwT_hi", [P, P], FP32R)
        hwT_lo = sb("hwT_lo", [P, P], FP32R)
        late = ctxq[:, 0, :, :].rearrange("p k n -> p (k n)").bitcast(FP32)
        xn = late[:, 0:2 * D].rearrange("p (i d) -> p i d", i=2)
        bias = late[:, 2 * D:3 * D]
        hw = late[:, 3 * D:3 * D + ER]
        ident16 = sb("ident16", [P, P], FP16)
        ident32 = sb("ident32", [P, P], FP32)
        ones16 = sb("ones16", [P, P], FP16)
        sc = sb("sc", [P, N_SCALARS + E], FP32)
        cc = sb("cc", [P, 12], FP32)
        th = sb("th", [P, 2], FP32)
        inv_k = sb("inv_k", [P, E], FP32)
        ones_e = sb("ones_e", [P, E], FP32)
        rowsum = sb("rowsum", [P, TILES], FP32)
        row_term = sb("row_term", [P, TILES], FP32)
        stats = sb("stats", [P, 2, NH, 6], FP32)
        mv = sb("mv", [P, 2, 2], FP32)
        var_e = sb("var_e", [P, 2], FP32)
        rs = sb("rs", [P, 2], FP32)
        sd = sb("sd", [P, 2], FP32)
        qa = sb("qa", [P, 2, 2], FP32)
        qm = sb("qm", [P, 2, 2], FP32)
        stats2 = sb("stats2", [P, 2, NH, 6], FP32)
        mv2 = sb("mv2", [P, 2, 2], FP32)
        var2 = sb("var2", [P, 2], FP32)
        rs2 = sb("rs2", [P, 2], FP32)
        minus_half = sb("minus_half", [P, 2], FP32)
        lg = sb("lg", [P, E], FP32)
        lg_sorted = sb("lg_sorted", [P, E], FP32)
        cum = sb("cum", [P, E], FP32)
        cand = sb("cand", [P, E], FP32)
        tau = sb("tau", [P, 1], FP32)
        ew = sb("ew", [P, E], FP32)

        S1, Z1, S2, Z2 = (sc[:, i:i + 1] for i in range(4))
        b_router = sc[:, N_SCALARS:N_SCALARS + E]
        INV1, INV2, NZS1, C, D1, D2, CD1, CD2, NKZ1, SS = (cc[:, i:i + 1] for i in range(10))
        TX, TF = th[:, 0:1], th[:, 1:2]

        acc = [[pb(f"acc{s}{n}", [P, HALF], FP32) for n in range(G)] for s in range(2)]
        xbank = [pb(f"xbank{n}", [P, HALF], FP32) for n in range(NH)]
        qbank = acc[0][2][:, :].bitcast(FP16).rearrange("p (k c) -> p k c", c=P)

        def first_bank(t):
            bank = acc[t % 2][FIRST]
            return bank[:, 0:ER], bank[:, ER:ARW], bank[:, HWT_AT:HWT_AT + P]

        small_in = sem("small_in")
        x_in = [sem(f"x_in{p}") for p in range(PAIRS)]
        ring_in = [sem(f"ring_in{s}") for s in range(RING)]
        tanh_ready = sem("tanh_ready")
        consts_ready = sem("consts_ready")
        ident_zero = sem("ident_zero")
        ident_ready = sem("ident_ready")
        bias_ready = sem("bias_ready")
        vec = sem("vec")
        ctx_rounded = [sem("ctx_rounded0"), sem("ctx_rounded1")]
        ctx_ready = sem("ctx_ready")
        q_rounded = sem("q_rounded")
        q16_ready = sem("q16_ready")
        q_turned = sem("q_turned")
        qT_ready = sem("qT_ready")
        attn_half = sem("attn_half")
        added = sem("added")
        colsum_done = sem("colsum_done")
        col_ready = sem("col_ready")
        w_hi_done = sem("w_hi_done")
        w_lo_done = [sem("w_lo_done_v"), sem("w_lo_done_g")]
        moments = sem("moments")
        q_scale = sem("q_scale")
        rows_ready = sem("rows_ready")
        moments2 = sem("moments2")
        rs2_ready = sem("rs2_ready")
        gp = sem("gp")
        xn_ready = sem("xn_ready")
        biased = sem("biased")
        x_turned = sem("x_turned")
        xT_hi_done = sem("xT_hi_done")
        xT_lo_done = sem("xT_lo_done")
        first_done = sem("first_done")
        hw_ready = sem("hw_ready")
        hw_turned = sem("hw_turned")
        hwT_hi_done = sem("hwT_hi_done")
        hwT_lo_done = sem("hwT_lo_done")
        layer_part = sem("layer_part")
        stored = sem("stored")

        block = stack.enter_context(nc.Block())

        def ring_ready(eng, i):
            eng.wait_ge(ring_in[i % RING], 16 * (i // RING + 1))

        def low_ready(eng, i):
            n = i - FIRST_W + 1
            eng.wait_ge(w_lo_done[0], min(n, BY_VECTOR))
            if n > BY_VECTOR:
                eng.wait_ge(w_lo_done[1], n - BY_VECTOR)

        def ring_part(i):
            kind, g, _ = items[i]
            slot = ring[:, i % RING, :]
            if kind == "w":
                width = CUTS[g + 1] - CUTS[g]
                return slot[:, 0:2 * width].rearrange("p (k c) -> p k c", c=width)
            return slot

        def split_out(i):
            kind, g, kp = items[i]
            if kind == "lb":
                return lb_hi[:, :], lb_lo[:, :]
            at = (slice(None), slice(2 * kp, 2 * kp + 2), slice(CUTS[g], CUTS[g + 1]))
            return w_hi[at], w_lo[at]

        LB_ITEM = FIRST_W + 2 * KP

        def w_item(g, kp):
            return FIRST_W + g * KP + kp + (g == THIRD)

        X_AFTER = {2: 1, KC + 1: 2, KC + 5: 3}

        @block.sync
        def _(sp):
            sp.dma_start(sc[:, :], scalars).then_inc(small_in, 16)
            sp.dma_start(xs[:, 0:2, :], x_rows[:, 0:2, :]).then_inc(x_in[0], 16)
            for i, (kind, a, b) in enumerate(items):
                j = i - RING
                if j >= FIRST_W:
                    low_ready(sp, j)
                elif j >= 0:
                    sp.wait_ge(ctx_rounded[j // KC], j % KC + 1)
                if kind == "ctx":
                    src = ctx_rows[:, a, b, :]
                elif kind == "lb":
                    src = lora_b
                else:
                    src = w_rows[:, 2 * b:2 * b + 2, CUTS[a]:CUTS[a + 1]]
                sp.dma_start(ring_part(i), src).then_inc(ring_in[i % RING], 16)
                if i in X_AFTER:
                    p = X_AFTER[i]
                    sp.dma_start(xs[:, 2 * p:2 * p + 2, :], x_rows[:, 2 * p:2 * p + 2, :]).then_inc(x_in[p], 16)
                if i == FIRST_W + KP:
                    sp.wait_ge(attn_half, NH * TPB)
                    sp.dma_start(bias[:, :], b_base.partition_broadcast(P)).then_inc(small_in, 16)
            (c1, _), (c2, _), (c3, _) = (group_cols(g) for g in range(G))
            early, late_cols = slice(c1.start, c2.stop), c3
            for t in range(TILES):
                for cols, n in ((early, 2), (late_cols, 3)):
                    sp.wait_ge(added, NH * TILES + G * t + n)
                    sp.dma_start(out_rows[:, t, cols], xs[:, t, cols]).then_inc(stored, 16)
            sp.wait_ge(stored, 16 * TILES * 2)

        @block.gpsimd
        def _(pool):
            pool.memset(ident16[:, :], 0.0).then_inc(ident_zero, 1)
            pool.memset(ident32[:, :], 0.0).then_inc(ident_zero, 1)
            pool.memset(ones16[:, :], 1.0).then_inc(ident_ready, 1)
            pool.wait_ge(ident_zero, 2)
            for m in (ident16, ident32):
                pool.affine_select(out=m[:, :], in_=m[:, :], compare_op=ALU.not_equal, fill=1.0, base=0,
                                   pattern=[[-1, P]], channel_multiplier=1).then_inc(ident_ready, 1)
            pool.memset(minus_half[:, :], -0.5).then_inc(gp, 1)
            step = [1]

            def then_wait(ins):
                step[0] += 1
                ins.then_inc(gp, 1)
                pool.wait_ge(gp, step[0])

            def q_scales(p):
                pool.wait_ge(moments, p + 1)
                then_wait(pool.tensor_scalar(var_e[:, :], mv[:, :, 1], 1.0, EPS, ALU.mult, ALU.add))
                then_wait(pool.tensor_tensor(rs[:, :], var_e[:, :], minus_half[:, :], ALU.pow))
                pool.tensor_scalar(qa[:, p % 2, :], rs[:, :], INV1, 1.0, ALU.mult, ALU.mult)
                then_wait(pool.tensor_tensor(sd[:, :], var_e[:, :], rs[:, :], ALU.mult))
                for i in range(2):
                    ins = pool.tensor_scalar(qm[:, p % 2, i:i + 1], sd[:, i:i + 1], NZS1, mv[:, i, 0:1],
                                             ALU.mult, ALU.add)
                ins.then_inc(q_scale, 1)

            def ctx_to_16(b, k):
                pool.wait_ge(ctx_rounded[b], k + 1)
                pool.tensor_scalar(ctxq[:, b, k, :], ctx_u8[:, k % 2, :], 1.0, -MID, ALU.mult, ALU.add)\
                    .then_inc(ctx_ready, 1)

            def rsqrt2(t):
                i = slice(t % 2, t % 2 + 1)
                pool.wait_ge(moments2, t + 1)
                then_wait(pool.tensor_scalar(var2[:, i], mv2[:, t % 2, 1:2], 1.0, EPS, ALU.mult, ALU.add))
                pool.tensor_tensor(rs2[:, i], var2[:, i], minus_half[:, 0:1], ALU.pow).then_inc(rs2_ready, 1)

            def add_bias(t):
                pool.wait_ge(xn_ready, t + 1)
                pool.tensor_tensor(xs[:, t, :], xs[:, t, :], bias[:, :], ALU.add).then_inc(biased, 1)

            def low_part(i):
                pool.wait_ge(w_hi_done, i - FIRST_W + 1)
                hi, lo = split_out(i)
                pool.tensor_tensor(lo, ring_part(i), hi.bitcast(FP32), ALU.subtract).then_inc(w_lo_done[1], 1)

            pool.wait_ge(consts_ready, 1)
            q_scales(0)
            for k in range(4):
                ctx_to_16(0, k)
            q_scales(1)
            for k in range(4, KC):
                ctx_to_16(0, k)
            for k in range(2):
                ctx_to_16(1, k)
            rsqrt2(0)
            rsqrt2(1)
            for k in range(2, 4):
                ctx_to_16(1, k)
            q_scales(2)
            for k in range(4, KC):
                ctx_to_16(1, k)
            q_scales(3)
            for i in range(FIRST_W + BY_VECTOR, len(items)):
                low_part(i)
            pool.wait_ge(bias_ready, 1)
            for t in range(2):
                add_bias(t)
            for t in range(2, TILES):
                rsqrt2(t)
                add_bias(t)

        @block.scalar
        def _(act):
            act.wait_ge(small_in, 16)
            act.activation(th[:, :], sc[:, 4:6], ACT.Tanh).then_inc(tanh_ready, 1)

            def q_to_16(t):
                act.wait_ge(q_rounded, t + 1)
                if t >= 2:
                    act.wait_ge(q_turned, t - 1)
                act.activation(q_16[:, t % 2, :], q_u8[:, t % 2, :], ACT.Copy,
                               accum_out=rowsum[:, t:t + 1]).then_inc(q16_ready, 1)

            def q_out(t):
                act.wait_ge(q_turned, t + 1)
                if t >= 2:
                    act.wait_ge(attn_half, NH * (t - 1))
                act.activation(qT[:, t % 2, :, :], qbank[:, :, :], ACT.Copy, bias=-MID).then_inc(qT_ready, 1)

            def col_out(b):
                act.wait_ge(colsum_done, b + 1)
                for n in range(NH):
                    act.activation(col_term[:, b, n * HALF:(n + 1) * HALF], xbank[n][:, :], ACT.Copy, scale=CD1)\
                       .then_inc(col_ready, 1)

            def round_ctx(b, k):
                i = b * KC + k
                ring_ready(act, i)
                act.wait_ge(ctx_ready, i - 1)
                act.activation(ctx_u8[:, k % 2, :], ring_part(i), ACT.Identity, bias=Z2, scale=INV2)\
                   .then_inc(ctx_rounded[b], 1)

            def high_part(i):
                hi, _ = split_out(i)
                ring_ready(act, i)
                act.activation(hi, ring_part(i), ACT.Copy).then_inc(w_hi_done, 1)

            act.wait_ge(consts_ready, 1)
            q_to_16(0)
            q_to_16(1)
            q_out(0)
            q_out(1)
            q_to_16(2)
            q_to_16(3)
            col_out(0)
            q_out(2)
            for k in range(KC // 2):
                round_ctx(1, k)
            q_out(3)
            for k in range(KC // 2, KC):
                round_ctx(1, k)
            for t in (4, 5):
                q_to_16(t)
            for t in (4, 5):
                q_out(t)
            q_to_16(6)
            q_to_16(7)
            col_out(1)
            q_out(6)
            for i in range(FIRST_W, FIRST_W + 3):
                high_part(i)
            q_out(7)

            def xT_high(t):
                for n in range(NH):
                    act.wait_ge(x_turned, NH * t + n + 1)
                    act.activation(xT_hi[:, t % 2, n * 4:(n + 1) * 4, :],
                                   xbank[n][:, :].rearrange("p (k c) -> p k c", c=P), ACT.Copy)\
                       .then_inc(xT_hi_done, 1)

            def hwT_high(t):
                act.wait_ge(hw_turned, t + 1)
                act.activation(hwT_hi[:, :], first_bank(t)[2], ACT.Copy).then_inc(hwT_hi_done, 1)

            xT_high(0)
            for i in range(FIRST_W + 3, len(items)):
                high_part(i)
            for t in range(TILES):
                hwT_high(t)
                if t + 1 < TILES:
                    xT_high(t + 1)

        @block.vector
        def _(dve):
            step = [0]

            def then_wait(ins):
                step[0] += 1
                ins.then_inc(vec, 1)
                dve.wait_ge(vec, step[0])

            for e in range(E):
                dve.memset(inv_k[:, e:e + 1], 1.0 / (e + 1))
            dve.memset(ones_e[:, :], 1.0)
            dve.wait_ge(small_in, 16)
            dve.wait_ge(tanh_ready, 1)
            dve.reciprocal(INV1, S1)
            dve.reciprocal(INV2, S2)
            dve.scalar_tensor_tensor(NZS1, Z1, -1.0, S1, ALU.mult, ALU.mult)
            dve.tensor_scalar(D1, Z1, -1.0, MID, ALU.mult, ALU.add)
            dve.tensor_scalar(D2, Z2, -1.0, MID, ALU.mult, ALU.add)
            dve.tensor_scalar(NKZ1, Z1, -float(D), None, ALU.mult)
            then_wait(dve.tensor_tensor(SS, S1, S2, ALU.mult))
            then_wait(dve.tensor_tensor(C, SS, TX, ALU.mult))
            dve.tensor_tensor(CD1, C, D1, ALU.mult)
            then_wait(dve.tensor_tensor(CD2, C, D2, ALU.mult))
            dve.tensor_copy(tau[:, :], CD2).then_inc(consts_ready, 1)

            def pair_moments(p):
                dve.wait_ge(x_in[p], 16)
                for i in range(2):
                    for n in range(NH):
                        ins = dve.bn_stats(stats[:, i, n, :], xs[:, 2 * p + i, n * HALF:(n + 1) * HALF])
                then_wait(ins)
                if p:
                    dve.wait_ge(q_scale, p)
                for i in range(2):
                    ins = dve.bn_aggr(mv[:, i, :], stats[:, i, :, :].rearrange("p n s -> p (n s)"))
                ins.then_inc(moments, 1)

            def quantise(p):
                dve.wait_ge(q_scale, p + 1)
                for i in range(2):
                    t = 2 * p + i
                    if t >= 2:
                        dve.wait_ge(q16_ready, t - 1)
                    dve.tensor_scalar(q_u8[:, i, :], xs[:, t, :], qm[:, p % 2, i:i + 1], qa[:, p % 2, i:i + 1],
                                      ALU.subtract, ALU.mult).then_inc(q_rounded, 1)

            def round_ctx(k):
                ring_ready(dve, k)
                if k >= 2:
                    dve.wait_ge(ctx_ready, k - 1)
                dve.tensor_scalar(ctx_u8[:, k % 2, :], ring_part(k), INV2, Z2, ALU.mult, ALU.add)\
                   .then_inc(ctx_rounded[0], 1)

            def add_attention(t):
                for n in range(NH):
                    cols = slice(n * HALF, (n + 1) * HALF)
                    dve.wait_ge(attn_half, NH * t + n + 1)
                    dve.scalar_tensor_tensor(xs[:, t, cols], acc[t % 2][n][:, :], C, xs[:, t, cols],
                                             ALU.mult, ALU.add).then_inc(added, 1)

            def row_terms(b):
                ts = slice(b * TPB, (b + 1) * TPB)
                dve.wait_ge(q16_ready, (b + 1) * TPB)
                dve.tensor_scalar(row_term[:, ts], rowsum[:, ts], NKZ1, CD2, ALU.add, ALU.mult).then_inc(rows_ready, 1)

            def norm_moments(t):
                b = t // TPB
                dve.wait_ge(col_ready, NH * (b + 1))
                dve.wait_ge(rows_ready, b + 1)
                dve.wait_ge(added, NH * (t + 1))
                then_wait(dve.scalar_tensor_tensor(xs[:, t, :], xs[:, t, :], row_term[:, t:t + 1],
                                                   col_term[:, b, :], ALU.add, ALU.add))
                for n in range(NH):
                    ins = dve.bn_stats(stats2[:, t % 2, n, :], xs[:, t, n * HALF:(n + 1) * HALF])
                then_wait(ins)
                dve.bn_aggr(mv2[:, t % 2, :], stats2[:, t % 2, :, :].rearrange("p n s -> p (n s)")).then_inc(moments2, 1)

            def normalise(t):
                dve.wait_ge(rs2_ready, t + 1)
                if t >= 2:
                    dve.wait_ge(x_turned, NH * (t - 1))
                else:
                    dve.wait_ge(attn_half, NH * TPB)
                dve.tensor_scalar(xn[:, t % 2, :], xs[:, t, :], mv2[:, t % 2, 0:1], rs2[:, t % 2:t % 2 + 1],
                                  ALU.subtract, ALU.mult).then_inc(xn_ready, 1)

            def low_part(i):
                dve.wait_ge(w_hi_done, i - FIRST_W + 1)
                hi, lo = split_out(i)
                dve.tensor_tensor(lo, ring_part(i), hi.bitcast(FP32), ALU.subtract).then_inc(w_lo_done[0], 1)

            def xT_low(t):
                for n in range(NH):
                    dve.wait_ge(xT_hi_done, NH * t + n + 1)
                    dve.tensor_tensor(xT_lo[:, t % 2, n * 4:(n + 1) * 4, :],
                                      xbank[n][:, :].rearrange("p (k c) -> p k c", c=P),
                                      xT_hi[:, t % 2, n * 4:(n + 1) * 4, :].bitcast(FP32), ALU.subtract)\
                       .then_inc(xT_lo_done, 1)

            def route(t):
                h_psum, lg_psum, _ = first_bank(t)
                dve.wait_ge(first_done, t + 1)
                then_wait(dve.tensor_tensor(lg[:, :], lg_psum, b_router, ALU.add))
                then_wait(dve.max(lg_sorted[:, :], lg[:, :]))
                then_wait(dve.tensor_tensor_scan(cum[:, :], ones_e[:, :], lg_sorted[:, :], -1.0,
                                                 ALU.mult, ALU.add))
                then_wait(dve.tensor_tensor(cand[:, :], cum[:, :], inv_k[:, :], ALU.mult))
                then_wait(dve.reduce_max(tau[:, :], cand[:, :], AX.X))
                then_wait(dve.tensor_scalar(ew[:, :], lg[:, :], tau[:, 0:1], 0.0, ALU.subtract, ALU.max))
                dve.tensor_tensor(hw[:, :].rearrange("p (e r) -> p e r", r=R),
                                  h_psum.rearrange("p (e r) -> p e r", r=R),
                                  ew[:, :].unsqueeze(2).to_broadcast([P, E, R]), ALU.mult).then_inc(hw_ready, 1)

            def hwT_low(t):
                dve.wait_ge(hwT_hi_done, t + 1)
                dve.tensor_tensor(hwT_lo[:, :], first_bank(t)[2], hwT_hi[:, :].bitcast(FP32), ALU.subtract)\
                   .then_inc(hwT_lo_done, 1)

            def add_layer(t, g, nth):
                cols, at = group_cols(g)
                dve.wait_ge(layer_part, G * t + nth)
                dve.scalar_tensor_tensor(xs[:, t, cols], acc[t % 2][g][:, at], TF, xs[:, t, cols],
                                         ALU.mult, ALU.add).then_inc(added, 1)

            pair_moments(0)
            for k in range(2):
                round_ctx(k)
            quantise(0)
            round_ctx(2)
            pair_moments(1)
            for k in range(3, 6):
                round_ctx(k)
            quantise(1)
            for k in range(6, KC):
                round_ctx(k)
            row_terms(0)
            add_attention(0)
            add_attention(1)
            norm_moments(0)
            norm_moments(1)
            add_attention(2)
            add_attention(3)
            normalise(0)
            normalise(1)
            pair_moments(2)
            quantise(2)
            pair_moments(3)
            quantise(3)
            row_terms(1)
            add_attention(4)
            add_attention(5)
            for i in range(FIRST_W, FIRST_W + 2):
                low_part(i)
            xT_low(0)
            for i in range(FIRST_W + 2, FIRST_W + 4):
                low_part(i)
            add_attention(6)
            for i in range(FIRST_W + 4, FIRST_W + BY_VECTOR):
                low_part(i)
            add_attention(7)
            dve.wait_ge(small_in, 32)
            dve.tensor_scalar(bias[:, :], bias[:, :], TF, None, ALU.mult).then_inc(bias_ready, 1)
            for t in range(TILES):
                route(t)
                hwT_low(t)
                if t + 2 < TILES:
                    norm_moments(t + 2)
                dve.wait_ge(biased, t + 1)
                add_layer(t, SECOND, 1)
                add_layer(t, FIRST, 2)
                if t + 1 < TILES:
                    xT_low(t + 1)
                if t + 2 < TILES:
                    normalise(t + 2)
                add_layer(t, THIRD, 3)

        @block.tensor
        def _(pe):
            pe.wait_ge(ident_ready, 3)

            def turn_q(t):
                pe.wait_ge(q16_ready, t + 1)
                if t:
                    pe.wait_ge(qT_ready, t)
                for k in range(KC):
                    ins = pe.transpose(qbank[:, k, :], q_16[:, t % 2, k * P:(k + 1) * P], ident16[:, :])
                ins.then_inc(q_turned, 1)

            def attend(t, n, k):
                return pe.matmul(acc[t % 2][n][:, :], qT[:, t % 2, k, :],
                                 ctxq[:, t // TPB, k, n * HALF:(n + 1) * HALF], start=(k == 0), stop=(k == KC - 1))

            def attend_first(b):
                t0 = b * TPB
                pe.wait_ge(qT_ready, t0 + 1)
                if b:
                    pe.wait_ge(added, NH * t0)
                    pe.wait_ge(col_ready, NH * b)
                for k in range(KC):
                    pe.wait_ge(ctx_ready, b * KC + k + 1)
                    for n in range(NH):
                        col = pe.matmul(xbank[n][:, :], ones16[:, :], ctxq[:, b, k, n * HALF:(n + 1) * HALF],
                                        start=(k == 0), stop=(k == KC - 1))
                    if k == KC - 1:
                        col.then_inc(colsum_done, 1)
                    for t in (t0, t0 + 1):
                        if k == 0 and t > t0:
                            pe.wait_ge(qT_ready, t + 1)
                        for n in range(NH):
                            ins = attend(t, n, k)
                            if k == KC - 1:
                                ins.then_inc(attn_half, 1)

            def attend_tile(t):
                pe.wait_ge(qT_ready, t + 1)
                pe.wait_ge(added, NH * (t - 1))
                for n in range(NH):
                    for k in range(KC):
                        ins = attend(t, n, k)
                    ins.then_inc(attn_half, 1)

            def turn_x(t):
                pe.wait_ge(xn_ready, t + 1)
                if t:
                    pe.wait_ge(xT_lo_done, NH * t)
                else:
                    pe.wait_ge(col_ready, NH * B)
                for k in range(KC):
                    ins = pe.transpose(xbank[k // 4][:, k % 4 * P:(k % 4 + 1) * P],
                                       xn[:, t % 2, k * P:(k + 1) * P], ident32[:, :])
                    if k % 4 == 3:
                        ins.then_inc(x_turned, 1)

            def layer(t, g, ks):
                cols = slice(CUTS[g], CUTS[g + 1])
                for k in ks:
                    if t == 0 and k % 2 == 0:
                        low_ready(pe, w_item(g, k // 2))
                    xh, xl = xT_hi[:, t % 2, k, :], xT_lo[:, t % 2, k, :]
                    for a, (l, r) in enumerate(((xl, w_hi), (xh, w_lo), (xh, w_hi))):
                        ins = pe.matmul(acc[t % 2][g][:, 0:CUTS[g + 1] - CUTS[g]], l, r[:, k, cols],
                                        start=(k == 0 and a == 0), stop=(k == KC - 1 and a == 2))
                return ins

            def experts(t, g):
                cols, at = group_cols(g)
                for l, r in ((hwT_lo, lb_hi), (hwT_hi, lb_lo), (hwT_hi, lb_hi)):
                    ins = pe.matmul(acc[t % 2][g][:, at], l[:, :], r[:, cols], start=False, stop=True,
                                    skip_group_check=True)
                ins.then_inc(layer_part, 1)

            turn_q(0)
            turn_q(1)
            attend_first(0)
            turn_q(2)
            turn_q(3)
            attend_tile(2)
            attend_tile(3)
            turn_q(4)
            turn_q(5)
            attend_first(1)
            turn_q(6)
            turn_q(7)
            turn_x(0)
            attend_tile(6)
            attend_tile(7)
            for t in range(TILES):
                if t == 0:
                    pe.wait_ge(added, NH * (TILES - 1))
                    pe.wait_ge(qT_ready, TILES)
                else:
                    pe.wait_ge(added, NH * TILES + G * (t - 1))
                pe.wait_ge(xT_lo_done, NH * (t + 1))
                layer(t, FIRST, range(KC)).then_inc(first_done, 1)
                layer(t, SECOND, range(KC - 2))
                pe.wait_ge(hw_ready, t + 1)
                pe.matmul(first_bank(t)[2], hw, ident32[:, :], is_transpose=True, start=False, stop=True,
                          skip_group_check=True).then_inc(hw_turned, 1)
                layer(t, SECOND, range(KC - 2, KC))
                pe.wait_ge(hwT_lo_done, t + 1)
                if t == 0:
                    low_ready(pe, LB_ITEM)
                experts(t, SECOND)
                experts(t, FIRST)
                if t + 1 < TILES:
                    turn_x(t + 1)
                layer(t, THIRD, range(KC))
                experts(t, THIRD)


def kernel(x, ctx_4096, g_xattn, g_ffn, L0_xattn_x1_scale, L0_xattn_x1_zp, L0_xattn_x2_scale, L0_xattn_x2_zp,
           L0_ffn_W_base, L0_ffn_b_base, L0_ffn_W_router, L0_ffn_b_router, L0_ffn_lora_A, L0_ffn_lora_B):
    import numpy as np
    import concourse.bacc as bacc
    from concourse.bass_utils import run_bass_kernel_spmd

    x = np.asarray(x)
    w_base, router = np.asarray(L0_ffn_W_base), np.asarray(L0_ffn_W_router)
    lora_a, lora_b = np.asarray(L0_ffn_lora_A), np.asarray(L0_ffn_lora_B)
    d_in = w_base.shape[1]
    scalars = np.concatenate([np.asarray(a).reshape(-1) for a in (
        L0_xattn_x1_scale, L0_xattn_x1_zp, L0_xattn_x2_scale, L0_xattn_x2_zp, g_xattn, g_ffn, L0_ffn_b_router)])
    arrays = {
        "x": x,
        "ctx": np.asarray(ctx_4096),
        "scalars": np.tile(scalars, (128, 1)),
        "weights": np.ascontiguousarray(np.concatenate(
            [lora_a.transpose(1, 0, 2).reshape(d_in, -1), router.T, w_base.T], axis=1)),
        "b_base": np.asarray(L0_ffn_b_base),
        "lora_b": np.ascontiguousarray(lora_b.reshape(-1, lora_b.shape[-1])),
    }
    nc = bacc.Bacc("TRN2", target_bir_lowering=False, num_devices=1)
    args = [nc.dram_tensor(f"in_{name}", a.shape, mybir.dt.from_np(a.dtype), kind="ExternalInput").ap()
            for name, a in arrays.items()]
    out = nc.dram_tensor("out_y", x.shape, mybir.dt.from_np(x.dtype), kind="ExternalOutput").ap()
    flamingo_layer(nc, *args, out)
    r = run_bass_kernel_spmd(nc, [{f"in_{name}": a for name, a in arrays.items()}], core_ids=[0])
    return r.results[0]["out_y"]
```

```python
import concourse.bass as bass
from concourse import mybir
from contextlib import ExitStack

FP32 = mybir.dt.float32
FP32R = mybir.dt.float32r
FP16 = mybir.dt.float16
UINT8 = mybir.dt.uint8
INT32 = mybir.dt.int32
ALU = mybir.AluOpType
ACT = mybir.ActivationFunctionType
AX = mybir.AxisListType

P = 128
HALF = 512
EPS = 1e-5
MID = 128.0
N_SCALARS = 6
RING = 5
U_SLOTS = 4
Q_SLOTS = 3


def flamingo_layer(nc, x, ctx, scalars, weights, b_base, lora_b, out):
    B, S, D = x.shape
    KC = D // P
    TILES = B * S // P
    TPB = S // P
    NH = D // HALF
    WC = weights.shape[1]
    ARW = WC - D
    ER = lora_b.shape[0]
    E = ARW - ER
    R = ER // E

    WIDE = 400
    CUTS = [0, WC - 2 * WIDE, WC - WIDE, WC]
    G = len(CUTS) - 1
    FIRST, SECOND, THIRD = range(G)
    HWT_AT = HALF - P
    assert CUTS[1] <= HWT_AT and ARW < CUTS[1]

    def group_cols(g):
        at = max(CUTS[g], ARW)
        return slice(at - ARW, CUTS[g + 1] - ARW), slice(at - CUTS[g], CUTS[g + 1] - CUTS[g])

    x_rows = x.rearrange("b (t p) d -> p (b t) d", p=P)
    out_rows = out.rearrange("b (t p) d -> p (b t) d", p=P)
    ctx_rows = ctx.rearrange("b (k p) n -> p b k n", p=P)
    w_rows = weights.rearrange("(k p) c -> p k c", p=P)

    KP = KC // 2
    items = [("ctx", b, k) for b in range(B) for k in range(KC)]
    items += [("w", g, kp) for g in (FIRST, SECOND) for kp in range(KP)]
    items += [("lb", 0, 0)] + [("w", THIRD, kp) for kp in range(KP)]
    FIRST_W = B * KC
    N_W = len(items) - FIRST_W
    LOW_BY = "GGGGGGVVVGGVG"
    ROUND_BY = "VSGSVVSS" "SSVSSSSS"
    QUANT_BY = "VVVVGGGV"
    assert len(LOW_BY) == N_W

    with ExitStack() as stack:
        def sb(name, shape, dt):
            return stack.enter_context(nc.sbuf_tensor(name, shape, dt))

        def pb(name, shape, dt):
            return stack.enter_context(nc.psum_tensor(name, shape, dt))

        def sem(name):
            return stack.enter_context(nc.semaphore(name))

        xs = sb("xs", [P, TILES, D], FP32)
        ring = sb("ring", [P, RING, D], FP32)
        ctx_u8 = sb("ctx_u8", [P, U_SLOTS, D], UINT8)
        ctxq = sb("ctxq", [P, B, KC, D], FP16)
        q_u8 = sb("q_u8", [P, 2, D], UINT8)
        q_16 = sb("q_16", [P, 2, D], FP16)
        qT = sb("qT", [P, Q_SLOTS, KC, P], FP16)
        col_term = sb("col_term", [P, B, D], FP32)
        w_hi = sb("w_hi", [P, KC, WC], FP32R)
        w_lo = sb("w_lo", [P, KC, WC], FP32R)
        lb_hi = sb("lb_hi", [P, D], FP32R)
        lb_lo = sb("lb_lo", [P, D], FP32R)
        xT_hi = sb("xT_hi", [P, 2, KC, P], FP32R)
        xT_lo = sb("xT_lo", [P, 2, KC, P], FP32R)
        hwT_hi = sb("hwT_hi", [P, P], FP32R)
        hwT_lo = sb("hwT_lo", [P, P], FP32R)
        late = ctxq[:, 0, :, :].rearrange("p k n -> p (k n)").bitcast(FP32)
        xn = late[:, 0:2 * D].rearrange("p (i d) -> p i d", i=2)
        bias = late[:, 2 * D:3 * D]
        hw = late[:, 3 * D:3 * D + ER]
        ctx_sum = [u8[:, 0:2, :].rearrange("p i d -> p (i d)").bitcast(FP16) for u8 in (ctx_u8, q_u8)]
        ident16 = sb("ident16", [P, P], FP16)
        ident32 = sb("ident32", [P, P], FP32)
        ones16 = sb("ones16", [P, P], FP16)
        sc = sb("sc", [P, N_SCALARS + E], FP32)
        cc = sb("cc", [P, 12], FP32)
        th = sb("th", [P, 2], FP32)
        inv_k = sb("inv_k", [P, E], FP32)
        ones_e = sb("ones_e", [P, E], FP32)
        rowsum = sb("rowsum", [P, TILES], FP32)
        row_term = sb("row_term", [P, TILES, 1], FP32)
        stats = sb("stats", [P, 2, NH, 6], FP32)
        mv = sb("mv", [P, 2, 2], FP32)
        var_e = sb("var_e", [P, 1], FP32)
        rs = sb("rs", [P, 1], FP32)
        sd = sb("sd", [P, 1], FP32)
        qa = sb("qa", [P, 2], FP32)
        qm = sb("qm", [P, 2], FP32)
        stats2 = sb("stats2", [P, 2, NH, 6], FP32)
        mv2 = sb("mv2", [P, 2, 2], FP32)
        var2 = sb("var2", [P, 2], FP32)
        rs2 = sb("rs2", [P, 2], FP32)
        minus_half = sb("minus_half", [P, 1], FP32)
        eps = sb("eps", [P, 1], FP32)
        lg = sb("lg", [P, E], FP32)
        lg_sorted = sb("lg_sorted", [P, E], FP32)
        cum = sb("cum", [P, E], FP32)
        cand = sb("cand", [P, E], FP32)
        tau = sb("tau", [P, 1], FP32)
        ew = sb("ew", [P, E], FP32)

        S1, Z1, S2, Z2 = (sc[:, i:i + 1] for i in range(4))
        b_router = sc[:, N_SCALARS:N_SCALARS + E]
        INV1, INV2, ZS1, C, D1, D2, CD1, CD2, NKZ1, SS = (cc[:, i:i + 1] for i in range(10))
        TX, TF = th[:, 0:1], th[:, 1:2]

        acc = [[pb(f"acc{s}{n}", [P, HALF], FP32) for n in range(G)] for s in range(2)]
        xbank = [pb(f"xbank{n}", [P, HALF], FP32) for n in range(NH)]
        qbank = [acc[i][THIRD][:, :].bitcast(FP16).rearrange("p (k c) -> p k c", c=P) for i in range(2)]

        def first_bank(i):
            bank = acc[i][FIRST]
            return bank[:, 0:ER], bank[:, ER:ARW], bank[:, HWT_AT:HWT_AT + P]

        small_in = sem("small_in")
        x0_first_half = sem("x0_first_half")
        x_in = [sem(f"x_in{t}") for t in range(TILES)]
        ring_in = [sem(f"ring_in{s}") for s in range(RING)]
        tanh_ready = sem("tanh_ready")
        consts_ready = sem("consts_ready")
        ident_zero = sem("ident_zero")
        ident_ready = sem("ident_ready")
        bias_ready = sem("bias_ready")
        vec = sem("vec")
        ctx_rounded = {"V": sem("ctx_rounded_v"),
                       "S": sem("ctx_rounded_s"),
                       "G": sem("ctx_rounded_g")}
        ctx_ready = sem("ctx_ready")
        q_rounded = {"V": sem("q_rounded_v"), "G": sem("q_rounded_g")}
        q16_ready = sem("q16_ready")
        q_turned = sem("q_turned")
        qT_ready = sem("qT_ready")
        attn_half = sem("attn_half")
        added = sem("added")
        chunks_added = [sem("chunks_added_g"), sem("chunks_added_v")]
        colsum_done = sem("colsum_done")
        col_ready = sem("col_ready")
        w_hi_done = sem("w_hi_done")
        w_lo_done = [sem("w_lo_done_v"), sem("w_lo_done_g")]
        moments = sem("moments")
        q_scale = sem("q_scale")
        rows_ready = sem("rows_ready")
        moments2 = sem("moments2")
        rs2_ready = sem("rs2_ready")
        gp = sem("gp")
        xn_ready = sem("xn_ready")
        biased = sem("biased")
        x_turned = sem("x_turned")
        xT_hi_done = sem("xT_hi_done")
        xT_lo_done = sem("xT_lo_done")
        first_done = sem("first_done")
        hw_ready = sem("hw_ready")
        hw_turned = sem("hw_turned")
        hwT_hi_done = sem("hwT_hi_done")
        hwT_lo_done = sem("hwT_lo_done")
        layer_part = sem("layer_part")
        stored = sem("stored")

        block = stack.enter_context(nc.Block())

        def tiles_of_layer(eng, tile, first=0):
            for t in range(first, 2):
                tile(t, t)
            with eng.Fori(2, TILES - 3, 2) as t:
                for i in range(2):
                    tile(t + i, i)
            for t in range(TILES - 2, TILES):
                tile(t, t % 2)

        def is_tile(t, which):
            return isinstance(t, int) and t == which

        def has_next(t, n):
            return not isinstance(t, int) or t + n < TILES

        def add_chunks(eng, half):
            first, total = half * KC // 2, ctx_sum[half]
            assert KC // 2 * MID <= 2048 and B == 2
            for k in range(1, KC // 2):
                if k > 1:
                    eng.wait_ge(chunks_added[half], k - 1)
                eng.tensor_tensor(total, ctxq[:, 1, first, :] if k == 1 else total, ctxq[:, 1, first + k, :],
                                  ALU.add).then_inc(chunks_added[half], 1)

        def ring_ready(eng, i):
            eng.wait_ge(ring_in[i % RING], 16 * (i // RING + 1))

        def low_ready(eng, i):
            done = LOW_BY[:i + 1]
            eng.wait_ge(w_lo_done[0], done.count("V"))
            if "G" in done:
                eng.wait_ge(w_lo_done[1], done.count("G"))

        def tile_is_rounded(eng, t):
            eng.wait_ge(q_rounded[QUANT_BY[t]], QUANT_BY[:t + 1].count(QUANT_BY[t]))

        def ctx_is_rounded(eng, i):
            eng.wait_ge(ctx_rounded[ROUND_BY[i]], ROUND_BY[:i + 1].count(ROUND_BY[i]))

        def ring_part(i):
            kind, g, _ = items[i]
            slot = ring[:, i % RING, :]
            if kind == "w":
                width = CUTS[g + 1] - CUTS[g]
                return slot[:, 0:2 * width].rearrange("p (k c) -> p k c", c=width)
            return slot

        def split_out(i):
            kind, g, kp = items[FIRST_W + i]
            if kind == "lb":
                return lb_hi[:, :], lb_lo[:, :]
            at = (slice(None), slice(2 * kp, 2 * kp + 2), slice(CUTS[g], CUTS[g + 1]))
            return w_hi[at], w_lo[at]

        LB_ITEM = 2 * KP

        def w_item(g, kp):
            return g * KP + kp + (g == THIRD)

        X_AFTER = {1: 2, 5: 3, 7: 4, 8: 5, 9: 6, 12: 7}

        @block.sync
        def _(sp):
            sp.dma_start(sc[:, :], scalars).then_inc(small_in, 16)
            for n in range(NH):
                cols = slice(n * HALF, (n + 1) * HALF)
                sp.dma_start(xs[:, 0, cols], x_rows[:, 0, cols])\
                  .then_inc(x0_first_half if n == 0 else x_in[0], 16)
            sp.dma_start(xs[:, 1, :], x_rows[:, 1, :]).then_inc(x_in[1], 16)
            for i, (kind, a, b) in enumerate(items):
                j = i - RING
                if j >= FIRST_W:
                    low_ready(sp, j - FIRST_W)
                elif j >= 0:
                    ctx_is_rounded(sp, j)
                if kind == "ctx":
                    src = ctx_rows[:, a, b, :]
                elif kind == "lb":
                    src = lora_b
                else:
                    src = w_rows[:, 2 * b:2 * b + 2, CUTS[a]:CUTS[a + 1]]
                sp.dma_start(ring_part(i), src).then_inc(ring_in[i % RING], 16)
                if i in X_AFTER:
                    t = X_AFTER[i]
                    sp.dma_start(xs[:, t, :], x_rows[:, t, :]).then_inc(x_in[t], 16)
                if i == FIRST_W + KP:
                    sp.wait_ge(attn_half, NH * TPB)
                    sp.dma_start(bias[:, :], b_base.partition_broadcast(P)).then_inc(small_in, 16)
            (c1, _), (c2, _), (c3, _) = (group_cols(g) for g in range(G))
            early, late_cols = slice(c1.start, c2.stop), c3
            with sp.Fori(0, TILES) as t:
                for cols, n in ((early, 2), (late_cols, 3)):
                    sp.wait_ge(added, NH * TILES + G * t + n)
                    sp.dma_start(out_rows[:, t, cols], xs[:, t, cols]).then_inc(stored, 16)
            sp.wait_ge(stored, 16 * TILES * 2)

        @block.gpsimd
        def _(pool):
            pool.memset(ident16[:, :], 0.0).then_inc(ident_zero, 1)
            pool.memset(ident32[:, :], 0.0).then_inc(ident_zero, 1)
            pool.memset(ones16[:, :], 1.0).then_inc(ident_ready, 1)
            pool.wait_ge(ident_zero, 2)
            for m in (ident16, ident32):
                pool.affine_select(out=m[:, :], in_=m[:, :], compare_op=ALU.not_equal, fill=1.0, base=0,
                                   pattern=[[-1, P]], channel_multiplier=1).then_inc(ident_ready, 1)
            pool.memset(minus_half[:, :], -0.5).then_inc(gp, 1)
            pool.memset(eps[:, :], EPS).then_inc(gp, 1)
            step = [2]

            def then_wait(ins):
                step[0] += 1
                ins.then_inc(gp, 1)
                pool.wait_ge(gp, step[0])

            def q_scales(t):
                i = slice(t % 2, t % 2 + 1)
                pool.wait_ge(moments, t + 1)
                then_wait(pool.tensor_scalar(var_e[:, :], mv[:, t % 2, 1:2], 1.0, EPS, ALU.mult, ALU.add))
                then_wait(pool.tensor_tensor(rs[:, :], var_e[:, :], minus_half[:, 0:1], ALU.pow))
                if t >= 2:
                    tile_is_rounded(pool, t - 2)
                pool.tensor_scalar(qa[:, i], rs[:, :], INV1, 1.0, ALU.mult, ALU.mult)
                then_wait(pool.tensor_tensor(sd[:, :], var_e[:, :], rs[:, :], ALU.mult))
                pool.tensor_scalar(qm[:, i], sd[:, :], ZS1, mv[:, t % 2, 0:1], ALU.mult, ALU.subtract)\
                    .then_inc(q_scale, 1)

            def round_ctx(b, k):
                i = b * KC + k
                assert ROUND_BY[i] == "G"
                ring_ready(pool, i)
                if i >= U_SLOTS:
                    pool.wait_ge(ctx_ready, i - U_SLOTS + 1)
                pool.tensor_scalar(ctx_u8[:, i % U_SLOTS, :], ring_part(i), INV2, Z2, ALU.mult, ALU.add)\
                    .then_inc(ctx_rounded["G"], 1)

            def quantise(t):
                assert QUANT_BY[t] == "G"
                pool.wait_ge(q_scale, t + 1)
                if t >= 2:
                    pool.wait_ge(q16_ready, t - 1)
                pool.tensor_scalar(q_u8[:, t % 2, :], xs[:, t, :], qm[:, t % 2:t % 2 + 1], qa[:, t % 2:t % 2 + 1],
                                   ALU.add, ALU.mult).then_inc(q_rounded["G"], 1)

            def ctx_to_16(b, k):
                ctx_is_rounded(pool, b * KC + k)
                pool.tensor_scalar(ctxq[:, b, k, :], ctx_u8[:, (b * KC + k) % U_SLOTS, :], 1.0, -MID, ALU.mult, ALU.add)\
                    .then_inc(ctx_ready, 1)

            def rsqrt2(t, i):
                pool.wait_ge(moments2, t + 1)
                then_wait(pool.tensor_tensor(var2[:, i:i + 1], mv2[:, i, 1:2], eps[:, :], ALU.add))
                pool.tensor_tensor(rs2[:, i:i + 1], var2[:, i:i + 1], minus_half[:, 0:1], ALU.pow)\
                    .then_inc(rs2_ready, 1)

            def add_half():
                pool.wait_ge(ctx_ready, B * KC)
                add_chunks(pool, 0)

            def add_bias(t):
                pool.wait_ge(xn_ready, t + 1)
                if is_tile(t, 0):
                    pool.wait_ge(bias_ready, 1)
                pool.tensor_tensor(xs[:, t, :], xs[:, t, :], bias[:, :], ALU.add).then_inc(biased, 1)

            def low_part(i):
                pool.wait_ge(w_hi_done, i + 1)
                hi, lo = split_out(i)
                pool.tensor_tensor(lo, ring_part(FIRST_W + i), hi.bitcast(FP32), ALU.subtract)\
                    .then_inc(w_lo_done[1], 1)

            pool.wait_ge(consts_ready, 1)
            q_scales(0)
            q_scales(1)
            ctx_to_16(0, 0)
            ctx_to_16(0, 1)
            round_ctx(0, 2)
            for k in range(2, 6):
                ctx_to_16(0, k)
            q_scales(2)
            q_scales(3)
            ctx_to_16(0, 6)
            ctx_to_16(0, 7)
            q_scales(4)
            quantise(4)
            ctx_to_16(1, 0)
            q_scales(5)
            quantise(5)
            for k in range(1, 4):
                ctx_to_16(1, k)
            q_scales(6)
            quantise(6)
            q_scales(7)
            ctx_to_16(1, 4)
            ctx_to_16(1, 5)
            rsqrt2(0, 0)
            ctx_to_16(1, 6)
            ctx_to_16(1, 7)
            rsqrt2(1, 1)
            for k in range(6):
                low_part(k)
            add_bias(0)
            low_part(9)
            add_bias(1)
            low_part(10)
            low_part(12)
            add_half()
            first_step = step[0]
            with pool.Fori(2, TILES - 1, 2) as t:
                for i in range(2):
                    step[0] = first_step + (t - 2) + i
                    rsqrt2(t + i, i)
                    add_bias(t + i)

        @block.scalar
        def _(act):
            act.wait_ge(small_in, 16)
            act.activation(th[:, :], sc[:, 4:6], ACT.Tanh).then_inc(tanh_ready, 1)

            def q_to_16(t):
                tile_is_rounded(act, t)
                if t >= 2:
                    act.wait_ge(q_turned, t - 1)
                act.activation(q_16[:, t % 2, :], q_u8[:, t % 2, :], ACT.Copy,
                               accum_out=rowsum[:, t:t + 1]).then_inc(q16_ready, 1)

            def q_out(t):
                act.wait_ge(q_turned, t + 1)
                if t >= Q_SLOTS:
                    act.wait_ge(attn_half, NH * (t - Q_SLOTS + 1))
                act.activation(qT[:, t % Q_SLOTS, :, :], qbank[t % 2][:, :, :], ACT.Copy, bias=-MID)\
                   .then_inc(qT_ready, 1)

            def col_out(b):
                act.wait_ge(colsum_done, b + 1)
                for n in range(NH):
                    act.activation(col_term[:, b, n * HALF:(n + 1) * HALF], xbank[n][:, :], ACT.Copy, scale=CD1)\
                       .then_inc(col_ready, 1)

            def round_ctx(b, k):
                i = b * KC + k
                assert ROUND_BY[i] == "S"
                ring_ready(act, i)
                if i >= U_SLOTS:
                    act.wait_ge(ctx_ready, i - U_SLOTS + 1)
                act.activation(ctx_u8[:, i % U_SLOTS, :], ring_part(i), ACT.Identity, bias=Z2, scale=INV2)\
                   .then_inc(ctx_rounded["S"], 1)

            def high_part(i):
                hi, _ = split_out(i)
                ring_ready(act, FIRST_W + i)
                act.activation(hi, ring_part(FIRST_W + i), ACT.Copy).then_inc(w_hi_done, 1)

            def xT_high(t, i):
                for n in range(NH):
                    act.wait_ge(x_turned, NH * t + n + 1)
                    act.activation(xT_hi[:, i, n * 4:(n + 1) * 4, :],
                                   xbank[n][:, :].rearrange("p (k c) -> p k c", c=P), ACT.Copy)\
                       .then_inc(xT_hi_done, 1)

            def hwT_high(t, i):
                act.wait_ge(hw_turned, t + 1)
                act.activation(hwT_hi[:, :], first_bank(i)[2], ACT.Copy).then_inc(hwT_hi_done, 1)

            act.wait_ge(consts_ready, 1)
            round_ctx(0, 1)
            q_to_16(0)
            q_to_16(1)
            q_out(0)
            q_out(1)
            round_ctx(0, 3)
            round_ctx(0, 6)
            q_to_16(2)
            round_ctx(0, 7)
            round_ctx(1, 0)
            q_to_16(3)
            q_out(2)
            col_out(0)
            q_out(3)
            round_ctx(1, 1)
            q_to_16(4)
            q_out(4)
            round_ctx(1, 3)
            q_to_16(5)
            round_ctx(1, 4)
            round_ctx(1, 5)
            q_out(5)
            round_ctx(1, 6)
            round_ctx(1, 7)
            q_to_16(6)
            q_to_16(7)
            high_part(0)
            high_part(1)
            q_out(6)
            for k in range(2, 5):
                high_part(k)
            xT_high(0, 0)
            q_out(7)
            for k in range(5, 11):
                high_part(k)
            hwT_high(0, 0)
            high_part(11)
            high_part(12)
            xT_high(1, 1)

            def layer_tile(t, i):
                hwT_high(t, i)
                if is_tile(t, 1):
                    col_out(1)
                if has_next(t, 1):
                    xT_high(t + 1, 1 - i)

            tiles_of_layer(act, layer_tile, first=1)

        @block.vector
        def _(dve):
            step = [0]

            def then_wait(ins, apart=False):
                step[0] += 1
                ins.then_inc(vec, 1)
                dve.wait_ge(vec, step[0])
                if apart and not isinstance(step[0], int):
                    dve.nop(nofuse=True)

            for e in range(E):
                dve.memset(inv_k[:, e:e + 1], 1.0 / (e + 1))
            dve.memset(ones_e[:, :], 1.0)
            dve.wait_ge(small_in, 16)
            dve.wait_ge(tanh_ready, 1)
            dve.reciprocal(INV1, S1)
            dve.reciprocal(INV2, S2)
            dve.tensor_tensor(ZS1, Z1, S1, ALU.mult)
            dve.tensor_scalar(D1, Z1, -1.0, MID, ALU.mult, ALU.add)
            dve.tensor_scalar(D2, Z2, -1.0, MID, ALU.mult, ALU.add)
            dve.tensor_scalar(NKZ1, Z1, -float(D), None, ALU.mult)
            then_wait(dve.tensor_tensor(SS, S1, S2, ALU.mult))
            then_wait(dve.tensor_tensor(C, SS, TX, ALU.mult))
            dve.tensor_tensor(CD1, C, D1, ALU.mult)
            then_wait(dve.tensor_tensor(CD2, C, D2, ALU.mult))
            dve.tensor_copy(tau[:, :], CD2).then_inc(consts_ready, 1)

            def tile_moments(t):
                if t >= 2:
                    dve.wait_ge(q_scale, t - 1)
                for n in range(NH):
                    dve.wait_ge(x0_first_half if (t, n) == (0, 0) else x_in[t], 16)
                    ins = dve.bn_stats(stats[:, t % 2, n, :], xs[:, t, n * HALF:(n + 1) * HALF])
                then_wait(ins)
                dve.bn_aggr(mv[:, t % 2, :], stats[:, t % 2, :, :].rearrange("p n s -> p (n s)"))\
                    .then_inc(moments, 1)

            def quantise(t):
                assert QUANT_BY[t] == "V"
                dve.wait_ge(q_scale, t + 1)
                if t >= 2:
                    dve.wait_ge(q16_ready, t - 1)
                dve.tensor_scalar(q_u8[:, t % 2, :], xs[:, t, :], qm[:, t % 2:t % 2 + 1], qa[:, t % 2:t % 2 + 1],
                                  ALU.add, ALU.mult).then_inc(q_rounded["V"], 1)

            def round_ctx(b, k):
                i = b * KC + k
                assert ROUND_BY[i] == "V"
                ring_ready(dve, i)
                if i >= U_SLOTS:
                    dve.wait_ge(ctx_ready, i - U_SLOTS + 1)
                dve.tensor_scalar(ctx_u8[:, i % U_SLOTS, :], ring_part(i), INV2, Z2, ALU.mult, ALU.add)\
                   .then_inc(ctx_rounded["V"], 1)

            def add_attention(t):
                for n in range(NH):
                    cols = slice(n * HALF, (n + 1) * HALF)
                    dve.wait_ge(attn_half, NH * t + n + 1)
                    dve.scalar_tensor_tensor(xs[:, t, cols], acc[t % 2][n][:, :], C, xs[:, t, cols],
                                             ALU.mult, ALU.add).then_inc(added, 1)

            def row_terms(b):
                ts = slice(b * TPB, (b + 1) * TPB)
                dve.wait_ge(q16_ready, (b + 1) * TPB)
                dve.tensor_scalar(row_term[:, ts, 0], rowsum[:, ts], NKZ1, CD2, ALU.add, ALU.mult)\
                    .then_inc(rows_ready, 1)

            def norm_moments(t, b, i):
                dve.wait_ge(col_ready, NH * (b + 1))
                dve.wait_ge(rows_ready, b + 1)
                dve.wait_ge(added, NH * (t + 1))
                then_wait(dve.scalar_tensor_tensor(xs[:, t, :], xs[:, t, :], row_term[:, t, :],
                                                   col_term[:, b, :], ALU.add, ALU.add), apart=True)
                for n in range(NH):
                    ins = dve.bn_stats(stats2[:, i, n, :], xs[:, t, n * HALF:(n + 1) * HALF])
                then_wait(ins, apart=True)
                dve.bn_aggr(mv2[:, i, :], stats2[:, i, :, :].rearrange("p n s -> p (n s)")).then_inc(moments2, 1)

            def normalise(t, i, free):
                dve.wait_ge(rs2_ready, t + 1)
                dve.wait_ge(*free)
                dve.tensor_scalar(xn[:, i, :], xs[:, t, :], mv2[:, i, 0:1], rs2[:, i:i + 1],
                                  ALU.subtract, ALU.mult).then_inc(xn_ready, 1)

            def low_part(i):
                dve.wait_ge(w_hi_done, i + 1)
                hi, lo = split_out(i)
                dve.tensor_tensor(lo, ring_part(FIRST_W + i), hi.bitcast(FP32), ALU.subtract)\
                    .then_inc(w_lo_done[0], 1)

            def xT_low(t, i):
                for n in range(NH):
                    dve.wait_ge(xT_hi_done, NH * t + n + 1)
                    dve.tensor_tensor(xT_lo[:, i, n * 4:(n + 1) * 4, :],
                                      xbank[n][:, :].rearrange("p (k c) -> p k c", c=P),
                                      xT_hi[:, i, n * 4:(n + 1) * 4, :].bitcast(FP32), ALU.subtract)\
                       .then_inc(xT_lo_done, 1)

            def scale_bias():
                dve.wait_ge(small_in, 32)
                dve.tensor_scalar(bias[:, :], bias[:, :], TF, None, ALU.mult).then_inc(bias_ready, 1)

            def route(t, i):
                h_psum, lg_psum, _ = first_bank(i)
                dve.wait_ge(first_done, t + 1)
                then_wait(dve.tensor_tensor(lg[:, :], lg_psum, b_router, ALU.add), apart=True)
                then_wait(dve.max(lg_sorted[:, :], lg[:, :]))
                then_wait(dve.tensor_tensor_scan(cum[:, :], ones_e[:, :], lg_sorted[:, :], -1.0,
                                                 ALU.mult, ALU.add))
                then_wait(dve.tensor_tensor(cand[:, :], cum[:, :], inv_k[:, :], ALU.mult))
                then_wait(dve.reduce_max(tau[:, :], cand[:, :], AX.X))
                then_wait(dve.tensor_scalar(ew[:, :], lg[:, :], tau[:, 0:1], 0.0, ALU.subtract, ALU.max))
                dve.tensor_tensor(hw[:, :].rearrange("p (e r) -> p e r", r=R),
                                  h_psum.rearrange("p (e r) -> p e r", r=R),
                                  ew[:, :].unsqueeze(2).to_broadcast([P, E, R]), ALU.mult).then_inc(hw_ready, 1)

            def hwT_low(t, i):
                dve.wait_ge(hwT_hi_done, t + 1)
                dve.tensor_tensor(hwT_lo[:, :], first_bank(i)[2], hwT_hi[:, :].bitcast(FP32), ALU.subtract)\
                   .then_inc(hwT_lo_done, 1)

            def add_half():
                dve.wait_ge(ctx_ready, B * KC)
                dve.wait_ge(q16_ready, TILES)
                add_chunks(dve, 1)

            def add_layer(t, i, g, nth):
                cols, at = group_cols(g)
                if g == SECOND:
                    dve.wait_ge(biased, t + 1)
                dve.wait_ge(layer_part, G * t + nth)
                dve.scalar_tensor_tensor(xs[:, t, cols], acc[i][g][:, at], TF, xs[:, t, cols],
                                         ALU.mult, ALU.add).then_inc(added, 1)

            tile_moments(0)
            tile_moments(1)
            quantise(0)
            round_ctx(0, 0)
            quantise(1)
            tile_moments(2)
            round_ctx(0, 4)
            round_ctx(0, 5)
            tile_moments(3)
            quantise(2)
            quantise(3)
            tile_moments(4)
            add_attention(0)
            tile_moments(5)
            row_terms(0)
            round_ctx(1, 2)
            add_attention(1)
            add_attention(2)
            tile_moments(6)
            tile_moments(7)
            add_attention(3)
            norm_moments(0, 0, 0)
            quantise(7)
            norm_moments(1, 0, 1)
            normalise(0, 0, (attn_half, NH * TPB))
            normalise(1, 1, (attn_half, NH * TPB))
            row_terms(1)
            add_attention(4)
            add_attention(5)
            xT_low(0, 0)
            add_attention(6)
            add_attention(7)
            scale_bias()
            low_part(6)
            low_part(7)
            route(0, 0)
            low_part(8)
            hwT_low(0, 0)
            norm_moments(2, 0, 0)
            low_part(11)
            add_layer(0, 0, SECOND, 1)
            add_layer(0, 0, FIRST, 2)
            xT_low(1, 1)
            add_layer(0, 0, THIRD, 3)
            add_half()
            normalise(2, 0, (x_turned, NH))
            STEPS = 8
            first_step = step[0] - STEPS

            def layer_tile(t, i):
                if has_next(t, 1):
                    step[0] = first_step + STEPS * t
                route(t, i)
                hwT_low(t, i)
                if has_next(t, 2):
                    norm_moments(t + 2, 1 if not isinstance(t, int) else (t + 2) // TPB, i)
                add_layer(t, i, SECOND, 1)
                add_layer(t, i, FIRST, 2)
                if has_next(t, 1):
                    xT_low(t + 1, 1 - i)
                if has_next(t, 2):
                    normalise(t + 2, i, (x_turned, NH * (t + 1)))
                add_layer(t, i, THIRD, 3)

            tiles_of_layer(dve, layer_tile, first=1)

        @block.tensor
        def _(pe):
            pe.wait_ge(ident_ready, 3)

            def turn_q(t):
                pe.wait_ge(q16_ready, t + 1)
                if t >= 2:
                    pe.wait_ge(qT_ready, t - 1)
                for k in range(KC):
                    ins = pe.transpose(qbank[t % 2][:, k, :], q_16[:, t % 2, k * P:(k + 1) * P], ident16[:, :])
                ins.then_inc(q_turned, 1)

            def attend(t, n, k):
                return pe.matmul(acc[t % 2][n][:, :], qT[:, t % Q_SLOTS, k, :],
                                 ctxq[:, t // TPB, k, n * HALF:(n + 1) * HALF], start=(k == 0), stop=(k == KC - 1))

            def sum_columns(k):
                pe.wait_ge(ctx_ready, k + 1)
                for n in range(NH):
                    ins = pe.matmul(xbank[n][:, :], ones16[:, :], ctxq[:, 0, k, n * HALF:(n + 1) * HALF],
                                    start=(k == 0), stop=(k == KC - 1))
                if k == KC - 1:
                    ins.then_inc(colsum_done, 1)

            def sum_last_batch():
                for half in range(2):
                    pe.wait_ge(chunks_added[half], KC // 2 - 1)
                    for n in range(NH):
                        ins = pe.matmul(xbank[n][:, :], ones16[:, :], ctx_sum[half][:, n * HALF:(n + 1) * HALF],
                                        start=(half == 0), stop=(half == 1))
                ins.then_inc(colsum_done, 1)

            def attend_chunk(t, k):
                if k == 0:
                    pe.wait_ge(qT_ready, t + 1)
                pe.wait_ge(ctx_ready, t // TPB * KC + k + 1)
                for n in range(NH):
                    if k == 0 and t >= 2:
                        pe.wait_ge(added, NH * (t - 2) + n + 1)
                    ins = attend(t, n, k)
                    if k == KC - 1:
                        ins.then_inc(attn_half, 1)

            def attend_even(b, k):
                attend_chunk(b * TPB, k)

            def attend_odd(b, k):
                attend_chunk(b * TPB + 1, k)

            def attend_tile(t):
                pe.wait_ge(qT_ready, t + 1)
                for n in range(NH):
                    pe.wait_ge(added, NH * (t - 2) + n + 1)
                    for k in range(KC):
                        ins = attend(t, n, k)
                    ins.then_inc(attn_half, 1)

            def turn_x(t, i, free):
                pe.wait_ge(xn_ready, t + 1)
                pe.wait_ge(*free)
                for k in range(KC):
                    ins = pe.transpose(xbank[k // 4][:, k % 4 * P:(k % 4 + 1) * P],
                                       xn[:, i, k * P:(k + 1) * P], ident32[:, :])
                    if k % 4 == 3:
                        ins.then_inc(x_turned, 1)

            def layer(t, i, g, ks):
                cols = slice(CUTS[g], CUTS[g + 1])
                for k in ks:
                    if is_tile(t, 0) and k % 2 == 0:
                        low_ready(pe, w_item(g, k // 2))
                    xh, xl = xT_hi[:, i, k, :], xT_lo[:, i, k, :]
                    for a, (l, r) in enumerate(((xl, w_hi), (xh, w_lo), (xh, w_hi))):
                        ins = pe.matmul(acc[i][g][:, 0:CUTS[g + 1] - CUTS[g]], l, r[:, k, cols],
                                        start=(k == 0 and a == 0), stop=(k == KC - 1 and a == 2))
                return ins

            def experts(i, g):
                cols, at = group_cols(g)
                for l, r in ((hwT_lo, lb_hi), (hwT_hi, lb_lo), (hwT_hi, lb_hi)):
                    ins = pe.matmul(acc[i][g][:, at], l[:, :], r[:, cols], start=False, stop=True,
                                    skip_group_check=True)
                ins.then_inc(layer_part, 1)

            sum_columns(0)
            turn_q(0)
            turn_q(1)
            attend_odd(0, 0)
            for k in range(1, 4):
                sum_columns(k)
            attend_odd(0, 1)
            for k in range(4):
                attend_even(0, k)
            for k in range(2, 5):
                attend_odd(0, k)
            sum_columns(4)
            attend_even(0, 4)
            attend_even(0, 5)
            turn_q(2)
            sum_columns(5)
            attend_odd(0, 5)
            sum_columns(6)
            attend_even(0, 6)
            attend_odd(0, 6)
            sum_columns(7)
            attend_even(0, 7)
            turn_q(3)
            attend_odd(0, 7)
            attend_tile(2)
            turn_q(4)
            attend_tile(3)
            turn_q(5)
            attend_even(1, 0)
            attend_even(1, 1)
            for k in range(4):
                attend_odd(1, k)
            attend_even(1, 2)
            turn_q(6)
            for k in range(3, 6):
                attend_even(1, k)
            attend_odd(1, 4)
            attend_even(1, 6)
            turn_q(7)
            turn_x(0, 0, (col_ready, NH))
            attend_even(1, 7)
            for k in range(5, KC):
                attend_odd(1, k)
            attend_tile(6)
            attend_tile(7)

            def layer_tile(t, i):
                if is_tile(t, 0):
                    pe.wait_ge(added, NH * (TILES - 1))
                    pe.wait_ge(qT_ready, TILES)
                else:
                    pe.wait_ge(added, NH * TILES + G * (t - 1))
                pe.wait_ge(xT_lo_done, NH * (t + 1))
                layer(t, i, FIRST, range(KC)).then_inc(first_done, 1)
                layer(t, i, SECOND, range(KC - 2))
                if is_tile(t, 1):
                    sum_last_batch()
                pe.wait_ge(hw_ready, t + 1)
                pe.matmul(first_bank(i)[2], hw, ident32[:, :], is_transpose=True, start=False, stop=True,
                          skip_group_check=True).then_inc(hw_turned, 1)
                layer(t, i, SECOND, range(KC - 2, KC))
                pe.wait_ge(hwT_lo_done, t + 1)
                if is_tile(t, 0):
                    low_ready(pe, LB_ITEM)
                experts(i, SECOND)
                experts(i, FIRST)
                if is_tile(t, 1):
                    pe.wait_ge(col_ready, NH * B)
                if has_next(t, 1):
                    turn_x(t + 1, 1 - i, (xT_lo_done, NH * (t + 1)))
                layer(t, i, THIRD, range(KC))
                experts(i, THIRD)

            tiles_of_layer(pe, layer_tile)


def kernel(x, ctx_4096, g_xattn, g_ffn, L0_xattn_x1_scale, L0_xattn_x1_zp, L0_xattn_x2_scale, L0_xattn_x2_zp,
           L0_ffn_W_base, L0_ffn_b_base, L0_ffn_W_router, L0_ffn_b_router, L0_ffn_lora_A, L0_ffn_lora_B):
    import numpy as np
    import concourse.bacc as bacc
    from concourse.bass_utils import run_bass_kernel_spmd

    x = np.asarray(x)
    w_base, router = np.asarray(L0_ffn_W_base), np.asarray(L0_ffn_W_router)
    lora_a, lora_b = np.asarray(L0_ffn_lora_A), np.asarray(L0_ffn_lora_B)
    d_in = w_base.shape[1]
    scalars = np.concatenate([np.asarray(a).reshape(-1) for a in (
        L0_xattn_x1_scale, L0_xattn_x1_zp, L0_xattn_x2_scale, L0_xattn_x2_zp, g_xattn, g_ffn, L0_ffn_b_router)])
    arrays = {
        "x": x,
        "ctx": np.asarray(ctx_4096),
        "scalars": np.tile(scalars, (128, 1)),
        "weights": np.ascontiguousarray(np.concatenate(
            [lora_a.transpose(1, 0, 2).reshape(d_in, -1), router.T, w_base.T], axis=1)),
        "b_base": np.asarray(L0_ffn_b_base),
        "lora_b": np.ascontiguousarray(lora_b.reshape(-1, lora_b.shape[-1])),
    }
    nc = bacc.Bacc("TRN2", target_bir_lowering=False, num_devices=1)
    args = [nc.dram_tensor(f"in_{name}", a.shape, mybir.dt.from_np(a.dtype), kind="ExternalInput").ap()
            for name, a in arrays.items()]
    out = nc.dram_tensor("out_y", x.shape, mybir.dt.from_np(x.dtype), kind="ExternalOutput").ap()
    flamingo_layer(nc, *args, out)
    r = run_bass_kernel_spmd(nc, [{f"in_{name}": a for name, a in arrays.items()}], core_ids=[0])
    return r.results[0]["out_y"]
```
